# Optimizing a Trainium2 kernel written in Bass

```python
import numpy as np
import jax
import jax.numpy as jnp

def _softmax(x, axis=-1):
    return jax.nn.softmax(x, axis=axis)

def _gelu(x):
    return jax.nn.gelu(x, approximate=True)

def _silu(x):
    return jax.nn.silu(x)

def _sigmoid(x):
    return jax.nn.sigmoid(x)

def _layernorm(x, axis=-1, eps=1e-05):
    m = jnp.mean(x, axis=axis, keepdims=True)
    v = jnp.var(x, axis=axis, keepdims=True)
    return (x - m) / jnp.sqrt(v + eps)

def _scatter_add(tgt, idx, src, axis=0):
    return tgt.at[idx].add(src)

def _segment_sum(src, seg, n):
    return jax.ops.segment_sum(src, seg, n)
kernel_name = 'mk_audio_tower_d1_tok_audfeat256_r4_5c4830'

def setup_inputs(seed: int=0):
    np.random.seed(seed)
    _w = jnp.asarray

    def _rec_inputs():
        import jax
        import jax.numpy as jnp
        _rk = jax.random.key(seed)
        x = -7.10856e-05 + 0.999911 * jax.random.normal(jax.random.fold_in(_rk, 1), (128, 375, 64), jnp.float32)
        return x
    x = _rec_inputs()

    def _L0_tok_setup():
        import jax, jax.numpy as jnp
        import numpy as np
        key = jax.random.key(seed)
        k1, k2 = jax.random.split(key)
        N, L, F = (32, 2048, 64)
        x = jax.random.normal(k1, (N, L, F), dtype=jnp.float32)
        W = jax.random.normal(k2, (F, F), dtype=jnp.float32) * (1.0 / np.sqrt(F))
        return {'x': x, 'W': W, 'pool_size': 4}
    _L0_tok_all = _L0_tok_setup()
    _L0_tok_in = {k: v for k, v in _L0_tok_all.items() if k in ('W',)}
    del _L0_tok_all

    def _L0_attn_setup():
        import jax, jax.numpy as jnp
        import numpy as np
        B, L, DIM = (8, 4096, 64)
        WINDOW, SHIFT, HEADS = (128, 64, 8)
        key = jax.random.key(seed)
        k0, k1, k2, k3 = jax.random.split(key, 4)
        x = jax.random.normal(k0, (B, L, DIM), dtype=jnp.float32)
        qkv_weight = jax.random.normal(k1, (3 * DIM, DIM), dtype=jnp.float32) * 0.02
        qkv_bias = jnp.zeros((3 * DIM,), dtype=jnp.float32)
        proj_weight = jax.random.normal(k2, (DIM, DIM), dtype=jnp.float32) * 0.02
        proj_bias = jnp.zeros((DIM,), dtype=jnp.float32)
        bias_table = jax.random.normal(k3, (2 * WINDOW - 1, HEADS), dtype=jnp.float32) * 0.02
        return {'x': x, 'qkv_weight': qkv_weight, 'qkv_bias': qkv_bias, 'proj_weight': proj_weight, 'proj_bias': proj_bias, 'bias_table': bias_table}
    _L0_attn_all = _L0_attn_setup()
    _L0_attn_in = {k: v for k, v in _L0_attn_all.items() if k in ('qkv_weight', 'qkv_bias', 'proj_weight', 'proj_bias', 'bias_table')}
    del _L0_attn_all

    def _L0_ffn_setup():
        import jax, jax.numpy as jnp
        import numpy as np
        B, T, IN_DIM = (64, 64, 64)
        HID, OUT_DIM = (128, 64)
        N_LAYERS, N_EXPERTS, N_SHARED = (2, 16, 1)
        key = jax.random.key(seed)
        ks = jax.random.split(key, 10)
        s = 0.02
        x = jax.random.normal(ks[0], (B, T, IN_DIM), dtype=jnp.float32)
        route_id = jax.random.randint(ks[1], (B,), 0, N_EXPERTS)
        Wi = jax.random.normal(ks[2], (HID, IN_DIM), dtype=jnp.float32) * s
        bi = jnp.zeros((HID,), dtype=jnp.float32)
        Wr = jax.random.normal(ks[3], (N_LAYERS, N_EXPERTS, HID, HID), dtype=jnp.float32) * s
        br = jax.random.normal(ks[4], (N_LAYERS, N_EXPERTS, HID), dtype=jnp.float32) * s
        Ws = jax.random.normal(ks[5], (N_LAYERS, N_SHARED, HID, HID), dtype=jnp.float32) * s
        bs = jax.random.normal(ks[6], (N_LAYERS, N_SHARED, HID), dtype=jnp.float32) * s
        Wo = jax.random.normal(ks[7], (OUT_DIM, HID), dtype=jnp.float32) * s
        bo = jnp.zeros((OUT_DIM,), dtype=jnp.float32)
        return {'x': x, 'route_id': route_id, 'Wi': Wi, 'bi': bi, 'Wr': Wr, 'br': br, 'Ws': Ws, 'bs': bs, 'Wo': Wo, 'bo': bo}
    _L0_ffn_all = _L0_ffn_setup()
    _L0_ffn_in = {k: v for k, v in _L0_ffn_all.items() if k in ('route_id', 'Wi', 'bi', 'Wr', 'br', 'Ws', 'bs', 'Wo', 'bo')}
    del _L0_ffn_all
    return {'x': x, 'L0_tok_W': _L0_tok_in['W'], 'L0_attn_qkv_weight': _L0_attn_in['qkv_weight'], 'L0_attn_qkv_bias': _L0_attn_in['qkv_bias'], 'L0_attn_proj_weight': _L0_attn_in['proj_weight'], 'L0_attn_proj_bias': _L0_attn_in['proj_bias'], 'L0_attn_bias_table': _L0_attn_in['bias_table'], 'L0_ffn_route_id': _L0_ffn_in['route_id'], 'L0_ffn_Wi': _L0_ffn_in['Wi'], 'L0_ffn_bi': _L0_ffn_in['bi'], 'L0_ffn_Wr': _L0_ffn_in['Wr'], 'L0_ffn_br': _L0_ffn_in['br'], 'L0_ffn_Ws': _L0_ffn_in['Ws'], 'L0_ffn_bs': _L0_ffn_in['bs'], 'L0_ffn_Wo': _L0_ffn_in['Wo'], 'L0_ffn_bo': _L0_ffn_in['bo']}

def reference(x, L0_tok_W, L0_attn_qkv_weight, L0_attn_qkv_bias, L0_attn_proj_weight, L0_attn_proj_bias, L0_attn_bias_table, L0_ffn_route_id, L0_ffn_Wi, L0_ffn_bi, L0_ffn_Wr, L0_ffn_br, L0_ffn_Ws, L0_ffn_bs, L0_ffn_Wo, L0_ffn_bo):
    import jax
    import jax.numpy as jnp

    def _L0_tok_ref(x, W, pool_size):
        import jax, jax.numpy as jnp
        import numpy as np
        N, L, F = x.shape
        p = int(pool_size)
        Lc = L - L % p
        xr = x[:, :Lc, :].reshape(N, Lc // p, p, F)
        raw = jnp.einsum('nlpf,fg->nlpg', xr, W)
        att = jax.nn.softmax(raw, axis=-2)
        return jnp.sum(xr * att, axis=-2)

    def _L0_attn_ref(x, qkv_weight, qkv_bias, proj_weight, proj_bias, bias_table):
        import jax, jax.numpy as jnp
        import numpy as np
        B, L, DIM = (8, 4096, 64)
        WINDOW, SHIFT, HEADS = (128, 64, 8)
        Bb, Ll, C = x.shape
        hd = C // HEADS
        pad = (WINDOW - Ll % WINDOW) % WINDOW
        xp = jnp.pad(x, ((0, 0), (0, pad), (0, 0)))
        pad_L = Ll + pad
        shift = 0 if WINDOW >= pad_L else SHIFT
        if shift > 0:
            xp = jnp.roll(xp, -shift, axis=1)
        nW = pad_L // WINDOW
        xw = xp.reshape(Bb * nW, WINDOW, C)
        qkv = xw @ qkv_weight.T + qkv_bias
        qkv = qkv.reshape(Bb * nW, WINDOW, 3, HEADS, hd).transpose(2, 0, 3, 1, 4)
        q, k, v = (qkv[0], qkv[1], qkv[2])
        scale = hd ** (-0.5)
        attn = jnp.einsum('whqd,whkd->whqk', q * scale, k)
        coords = jnp.arange(WINDOW)
        rel_idx = coords[:, None] - coords[None, :] + WINDOW - 1
        rpb = bias_table[rel_idx]
        attn = attn + jnp.transpose(rpb, (2, 0, 1))[None]
        if shift > 0:
            region = jnp.zeros((pad_L,), dtype=x.dtype)
            region = region.at[pad_L - WINDOW:pad_L - shift].set(1.0)
            region = region.at[pad_L - shift:].set(2.0)
            region = region.reshape(nW, WINDOW)
            mask = jnp.where(region[:, None, :] != region[:, :, None], -100.0, 0.0).astype(x.dtype)
            attn = attn.reshape(Bb, nW, HEADS, WINDOW, WINDOW) + mask[None, :, None]
            attn = attn.reshape(Bb * nW, HEADS, WINDOW, WINDOW)
        attn = jax.nn.softmax(attn, axis=-1)
        out = jnp.einsum('whqk,whkd->wqhd', attn, v).reshape(Bb * nW, WINDOW, C)
        out = out @ proj_weight.T + proj_bias
        out = out.reshape(Bb, pad_L, C)
        if shift > 0:
            out = jnp.roll(out, shift, axis=1)
        return out[:, :Ll, :]

    def _L0_ffn_ref(x, route_id, Wi, bi, Wr, br, Ws, bs, Wo, bo):
        import jax, jax.numpy as jnp
        import numpy as np
        B, T, IN_DIM = (64, 64, 64)
        HID, OUT_DIM = (128, 64)
        N_LAYERS, N_EXPERTS, N_SHARED = (2, 16, 1)
        flat = x.reshape(-1, x.shape[-1])
        n_tok = flat.shape[0]
        route = jnp.repeat(route_id, n_tok // route_id.shape[0])
        h = jax.nn.relu(flat @ Wi.T + bi)
        n_layers, n_experts = (Wr.shape[0], Wr.shape[1])
        for l in range(n_layers):
            shared = (jnp.einsum('nd,shd->snh', h, Ws[l]) + bs[l][:, None, :]).mean(axis=0)
            routed = jnp.zeros_like(h)
            for e in range(n_experts):
                ye = h @ Wr[l, e].T + br[l, e]
                routed = routed + jnp.where((route == e)[:, None], ye, 0.0)
            h = jax.nn.relu(shared + routed + h)
        out = h @ Wo.T + bo
        return out.reshape(*x.shape[:-1], out.shape[-1])
    h = _L0_tok_ref(x, L0_tok_W, 4)
    h = h + _L0_attn_ref(_layernorm(h, axis=-1), L0_attn_qkv_weight, L0_attn_qkv_bias, L0_attn_proj_weight, L0_attn_proj_bias, L0_attn_bias_table)
    h = h + _L0_ffn_ref(_layernorm(h, axis=-1), L0_ffn_route_id, L0_ffn_Wi, L0_ffn_bi, L0_ffn_Wr, L0_ffn_br, L0_ffn_Ws, L0_ffn_bs, L0_ffn_Wo, L0_ffn_bo)
    return h

_drawn_inputs = setup_inputs


def setup_inputs(seed=0):
    import zlib

    import numpy as np

    out = dict(_drawn_inputs(seed))
    spreads = {'L0_attn_qkv_bias': (0.0, 0.28),
     'L0_attn_proj_bias': (0.0, 0.1),
     'L0_ffn_bi': (0.0, 0.319),
     'L0_ffn_bo': (0.0, 0.1)}
    factors = {'L0_attn_qkv_weight': 8.0,
     'L0_attn_bias_table': 47.834,
     'L0_ffn_Wr': 4.522,
     'L0_ffn_br': 7.511,
     'L0_ffn_Ws': 4.505,
     'L0_ffn_bs': 6.886}
    for name, (base, spread) in spreads.items():
        noise = np.random.default_rng([zlib.crc32(name.encode()), seed]).standard_normal(out[name].shape)
        drawn = base * np.exp(spread * noise) if base else spread * noise
        out[name] = jnp.asarray(drawn.astype(out[name].dtype))
    for name, factor in factors.items():
        out[name] = (out[name] * factor).astype(out[name].dtype)
    return out
```

```python
from contextlib import ExitStack

import numpy as np

import concourse.bass as bass
from concourse import mybir

F32 = mybir.dt.float32
BF16 = mybir.dt.bfloat16
I32 = mybir.dt.int32
ACT = mybir.ActivationFunctionType
ALU = mybir.AluOpType
AX_X = mybir.AxisListType.X

B, D = 128, 64
POOL = 4
T = 375 // POOL
WINDOW = 128
PADDED = WINDOW - T
C = 96
K = T + 1
HEADS, HD = 8, 8
HH, QG = 4, 2
HID, LAYERS = 128, 2
PAIRS = 4
SLOTS = 2 * PAIRS
GROUPS = B // SLOTS
RAW = POOL * T
N = PAIRS * C
NB = HH * C
NT = 2 * WINDOW - 1
WC = HID + 1
ROWS_Q = 32
ROWS_K = 33
VB = QG * HH * 40
SCALE = HD ** -0.5
EPS = 1e-5

W_TOK, W_QK, W_V, W_P, W_I, W_O = 0, 128, 384, 512, 640, 896
W_S = 960
W_BIAS = W_S + LAYERS * WC
W_BV = W_BIAS + 4
W_ALL = W_BV + D
C_CEN, C_MEAN, C_ID, C_ONES, C_FLIP, C_ALL = 0, 128, 256, 384, 512, 512 + C


def two_by_two(eng, first, last, step):
    with eng.Fori(first // 2, last // 2) as i:
        for par in range(2):
            step(2 * i + par, par)


def build(nc, xT, weights, consts, id16, key_rows, zeros, tab, tab_rev, experts, route, outT):
    with ExitStack() as ctx:
        def sb(name, shape, dt=F32):
            return ctx.enter_context(nc.sbuf_tensor(name, shape, dt))

        def sem(name):
            return ctx.enter_context(nc.semaphore(name))

        bank = [ctx.enter_context(nc.psum_tensor(f"bank{i}", [128, 512], F32)) for i in range(8)]

        wts = sb("wts", [128, W_ALL])
        cst = sb("cst", [128, C_ALL])
        neg_id = sb("neg_id", [128, 128], BF16)
        route_sb = sb("route_sb", [1, B // 2], I32)
        bq_scaled = sb("bq_scaled", [64, 1])
        eps_col = sb("eps_col", [128, 1])
        shared = sb("shared", [128, LAYERS * WC])
        rel_q16 = sb("rel_q16", [C, HEADS, C], BF16)
        pad_bias = sb("pad_bias", [C, HEADS, PADDED])
        pad_max = sb("pad_max", [C, HEADS])
        pad_sum = sb("pad_sum", [C, HEADS])
        pad_lse = sb("pad_lse", [C, HEADS])
        pad_rows = sb("pad_rows", [HEADS, C])

        H = sb("H", [128, GROUPS, PAIRS, C])
        XH = sb("XH", [128, GROUPS, PAIRS, C])
        SQ = sb("SQ", [128, N])
        LOGV = sb("LOGV", [128, N])
        RSTD = sb("RSTD", [128, N])

        A = sb("A", [128, 2, SLOTS, QG, C])
        BQ = sb("BQ", [128, 2, SLOTS, QG, HH, C])
        AQ = sb("AQ", [128, SLOTS, QG, C], BF16)
        BK = sb("BK", [128, SLOTS, QG, HH, C], BF16)
        staging = sb("staging", [128, 2, SLOTS * C])
        q_st = staging[0:64].rearrange("p g (s c) -> p g s c", s=SLOTS)
        rel_q = staging[0:C, 0].rearrange("p (h c) -> p h c", h=HEADS)
        rel_k = staging[0:K, 1].rearrange("p (h c) -> p h c", h=HEADS)
        k_st = sb("k_st", [128, SLOTS, C], BF16)
        XS = sb("XS", [128, PAIRS, C])
        Vm = sb("Vm", [128, 2, SLOTS * VB])
        mx = sb("mx", [C, 2, SLOTS * HEADS])
        neg_max = sb("neg_max", [32, 2, 2, C])
        RDEN = sb("RDEN", [128, 2, C])

        M16 = sb("M16", [128, PAIRS, T], BF16)
        ND = sb("ND", [128, 2, PAIRS, T])
        RD = sb("RD", [128, PAIRS, T])
        region = sb("region", [128, 4 * PAIRS * RAW])
        XR = region[:, 0:2 * PAIRS * RAW].rearrange("p (g n f) -> p g n f", g=2, n=PAIRS)
        EX = region[:, 2 * PAIRS * RAW:4 * PAIRS * RAW].rearrange("p (g n f) -> p g n f", g=2, n=PAIRS)
        P = region[:, 0:2 * 2 * QG * NB].rearrange("p (n s g f) -> p n s g f", n=2, s=2, g=QG)
        at = [0]

        def part(cols):
            at[0] += cols
            return region[:, at[0] - cols:at[0]]

        WR = part(2 * PAIRS * LAYERS * WC).rearrange("p (g n f) -> p g n f", g=2, n=PAIRS)
        R0, R1, R2 = (part(2 * N).rearrange("p (n s c) -> p n s c", n=PAIRS, s=2) for _ in range(3))
        X2 = part(N)
        OUT = part(2 * N).rearrange("p (g n c) -> p g n c", g=2, n=PAIRS)

        weights_in, route_in, bias_in = sem("weights_in"), sem("route_in"), sem("bias_in")
        pad_shifted, pad_exp, pad_summed, pad_logged, pad_done = (
            sem("pad_shifted"), sem("pad_exp"), sem("pad_summed"), sem("pad_logged"), sem("pad_done"))
        pad_maxed, rel16_cast, rel16_done = sem("pad_maxed"), sem("rel16_cast"), sem("rel16_done")
        pad_flipped, pad_turned = sem("pad_flipped"), sem("pad_turned")
        pad_row_in, zeros_in, rows_in = sem("pad_row_in"), sem("zeros_in"), sem("rows_in")
        small_ready, shared_copied, shared_ready = sem("small_ready"), sem("shared_copied"), sem("shared_ready")
        pads_zeroed, probs_zeroed = sem("pads_zeroed"), sem("probs_zeroed")
        x_in = [sem("x_in0"), sem("x_in1")]
        raw_ready, max_ready, shift_ready = sem("raw_ready"), sem("max_ready"), sem("shift_ready")
        exp_ready, prod_ready, ehalf_ready = sem("exp_ready"), sem("prod_ready"), sem("ehalf_ready")
        xhalf_ready, sums_ready, recip_ready, h_ready = (
            sem("xhalf_ready"), sem("sums_ready"), sem("recip_ready"), sem("h_ready"))
        cen_ready, sq_ready, var_ready, log_ready, rstd_ready, xh_ready = (
            sem("cen_ready"), sem("sq_ready"), sem("var_ready"), sem("log_ready"), sem("rstd_ready"), sem("xh_ready"))
        qk_ready, xs_ready, v_ready, vm_ready = sem("qk_ready"), sem("xs_ready"), sem("v_ready"), sem("vm_ready")
        k16_ready, aq_ready, q_ready, key_ready = sem("k16_ready"), sem("aq_ready"), sem("q_ready"), sem("key_ready")
        kdiag_in, qdiag_in, negmax_in = sem("kdiag_in"), sem("qdiag_in"), sem("negmax_in")
        mx_filled, mx_read, negmax_ready = sem("mx_filled"), sem("mx_read"), sem("negmax_ready")
        s_ready, p_ready, od_ready, rden_ready, attn_ready = (
            sem("s_ready"), sem("p_ready"), sem("od_ready"), sem("rden_ready"), sem("attn_ready"))
        expert_in, expert_ready = [sem("expert_in0"), sem("expert_in1")], sem("expert_ready")
        proj_ready, h2_ready, cen2_ready, sq2_ready, var2_ready, log2_ready, rstd2_ready, x2_ready = (
            sem("proj_ready"), sem("h2_ready"), sem("cen2_ready"), sem("sq2_ready"), sem("var2_ready"),
            sem("log2_ready"), sem("rstd2_ready"), sem("x2_ready"))
        wi_ready, r0_ready, l1_ready, r1_ready, l2_ready, r2_ready = (
            sem("wi_ready"), sem("r0_ready"), sem("l1_ready"), sem("r1_ready"), sem("l2_ready"), sem("r2_ready"))
        wo_ready, out_ready = sem("wo_ready"), sem("out_ready")
        out_stored = [sem("out_stored0"), sem("out_stored1")]

        block = ctx.enter_context(nc.Block())
        w_tok, w_v, w_p = wts[:, W_TOK:W_TOK + 128], wts[:, W_V:W_V + 128], wts[:, W_P:W_P + 128]
        w_qk = [wts[:, W_QK + 128 * s:W_QK + 128 * (s + 1)] for s in range(2)]
        w_i = [wts[:, W_I + 128 * s:W_I + 128 * (s + 1)] for s in range(2)]
        w_o = wts[:, W_O:W_O + D]
        b_qk, b_p, b_i, b_o = (wts[:, W_BIAS + i:W_BIAS + i + 1] for i in range(4))
        b_v = wts[0:K, W_BV:W_BV + D]
        centre, mean, ident = cst[:, C_CEN:C_CEN + 128], cst[:, C_MEAN:C_MEAN + 128], cst[:, C_ID:C_ID + 128]
        ones_head = [cst[:, C_ONES + 32 * hh:C_ONES + 32 * (hh + 1)] for hh in range(HH)]

        bank_max, bank_s = [bank[3], bank[4]], [bank[5], bank[6]]
        OD = bank[7][:, 0:2 * C].rearrange("p (k c) -> p k c", k=2)

        MAX_ITEMS = 4 * PAIRS + 2
        T0_AT = 10

        @block.sync
        def _(sp):
            sp.dma_start(wts[:], weights).then_inc(weights_in, 16)
            sp.dma_start(XR[:, 0], xT[0]).then_inc(x_in[0], 16)
            sp.dma_start(cst[:], consts).then_inc(weights_in, 16)
            sp.dma_start(neg_id[:], id16[:, 0:128]).then_inc(weights_in, 16)
            sp.dma_start(XR[:, 1], xT[1]).then_inc(x_in[1], 16)
            sp.dma_start(pad_bias[:], bass.AP(tab_rev.tensor, WINDOW - C + T, [[1, C], [NT, HEADS], [1, PADDED]])
                         ).then_inc(bias_in, 16)
            sp.dma_start(rel_q, bass.AP(tab_rev.tensor, WINDOW - C, [[1, C], [NT, HEADS], [1, C]])
                         ).then_inc(bias_in, 16)
            sp.dma_start(rel_k[0:T], bass.AP(tab.tensor, WINDOW - T, [[1, T], [NT, HEADS], [1, C]])
                         ).then_inc(bias_in, 16)
            sp.dma_start(route_sb[:], route).then_inc(route_in, 16)
            zero_rows = [(A[0:32], 2 * SLOTS * QG * C), (BQ[0:33], 2 * SLOTS * QG * NB), (Vm[:], 2 * SLOTS * VB)]
            for dst, cols in zero_rows:
                rows = dst.shape[0]
                flat = dst.rearrange("p a s g c -> p (a s g c)") if len(dst.shape) == 5 else (
                    dst.rearrange("p a s g h c -> p (a s g h c)") if len(dst.shape) == 6 else
                    dst.rearrange("p a c -> p (a c)"))
                sp.dma_start(flat, bass.AP(zeros.tensor, 0, [[0, rows], [1, cols]])).then_inc(zeros_in, 16)
            sp.dma_start(BK[0:32].rearrange("p s g h c -> p (s g h c)").bitcast(F32),
                         bass.AP(zeros.tensor, 0, [[0, 32], [1, SLOTS * QG * NB // 2]])).then_inc(zeros_in, 16)
            sp.dma_start(A[32:33 + K].rearrange("p a s g c -> p (a s g) c"),
                         bass.AP(key_rows.tensor, 0, [[C, K + 1], [0, 2 * SLOTS * QG], [1, C]])).then_inc(rows_in, 16)
            sp.dma_start(AQ[ROWS_Q:128].rearrange("p s g c -> p (s g) c"),
                         bass.AP(id16.tensor, 128, [[128 + C, C], [0, SLOTS * QG], [1, C]])).then_inc(rows_in, 16)
            sp.wait_ge(pad_turned, 1)
            sp.dma_start(rel_k[T:K], pad_rows[:]).then_inc(pad_row_in, 16)
            sp.wait_ge(rel16_done, 1)
            for s in range(SLOTS):
                sp.dma_start(BK[ROWS_Q:128, s].rearrange("p g h c -> p (g h) c"), rel_q16[:]
                             ).then_inc(rows_in, 16)
            sp.wait_ge(pad_row_in, 16)
            sp.wait_ge(bias_in, 48)
            for par in range(2):
                for s in range(SLOTS):
                    sp.dma_start(BQ[ROWS_K:ROWS_K + K, par, s].rearrange("p g h c -> p (g h) c"), rel_k
                                 ).then_inc(rows_in, 16)

            def load_x(g, par):
                sp.wait_ge(sums_ready, g - 1)
                sp.dma_start(XR[:, par], xT[g]).then_inc(x_in[par], 16)

            two_by_two(sp, 2, GROUPS, load_x)

            def key_diagonals(g, par):
                sp.wait_ge(k16_ready, 2 * (g + 1))
                for h in range(HEADS):
                    hh, qg = h % HH, h // HH
                    sp.dma_start(BK[HD * hh:HD * (hh + 1), :, qg, hh, :], k_st[64 + HD * h:64 + HD * (h + 1)]
                                 ).then_inc(kdiag_in, 16)

            def query_diagonals(g, par):
                sp.wait_ge(q_ready, 2 * (g + 1))
                for h in range(HEADS):
                    hh, qg = h % HH, h // HH
                    sp.dma_start(BQ[HD * hh:HD * (hh + 1), par, :, qg, hh, :], q_st[HD * h:HD * (h + 1), par]
                                 ).then_inc(qdiag_in, 16)

            def negmax(g, par, half):
                sp.wait_ge(negmax_ready, 2 * g + half + 1)
                sp.dma_start(BQ[32:33, par, 4 * half:4 * (half + 1)].rearrange("o s g h c -> o (s g h) c"),
                             neg_max[:, par, half]).then_inc(negmax_in, 16)

            def attention(g, par, more=True):
                if more:
                    key_diagonals(g + 1, 1 - par)
                negmax(g, par, 1)
                if more:
                    query_diagonals(g + 1, 1 - par)
                    negmax(g + 1, 1 - par, 0)

            sp.wait_ge(rows_in, 16 * (2 + 3 * SLOTS))
            sp.wait_ge(zeros_in, 64)
            key_diagonals(0, 0)
            query_diagonals(0, 0)
            negmax(0, 0, 0)
            two_by_two(sp, 0, GROUPS - 2, attention)
            attention(GROUPS - 2, 0)
            attention(GROUPS - 1, 1, more=False)

            def load_experts(g, par, first=False):
                if not first:
                    sp.wait_ge(r2_ready, PAIRS * (g - 1))
                for n in range(PAIRS):
                    r = sp.value_load(route_sb[0:1, bass.ds(PAIRS * g + n, 1)], min_val=0, max_val=15)
                    sp.dma_start(WR[:, par, n], experts[r]).then_inc(expert_in[par], 16)

            def store(g, par):
                sp.wait_ge(out_ready, g + 1)
                sp.dma_start(outT[g], OUT[:, par, :, 0:T]).then_inc(out_stored[par], 16)

            def mlp(g, par):
                load_experts(g + 2, par)
                store(g, par)

            sp.wait_ge(route_in, 16)
            sp.wait_ge(od_ready, PAIRS * GROUPS)
            load_experts(0, 0, first=True)
            load_experts(1, 1, first=True)
            two_by_two(sp, 0, GROUPS - 2, mlp)
            store(GROUPS - 2, 0)
            store(GROUPS - 1, 1)
            for par in range(2):
                sp.wait_ge(out_stored[par], 16 * GROUPS // 2)

        @block.gpsimd
        def _(pool):
            pool.memset(H[:, :, :, T:C], 0.0).then_inc(pads_zeroed, 1)
            pool.wait_ge(weights_in, 48)
            pool.tensor_copy(shared[:], wts[:, W_S:W_S + LAYERS * WC]).then_inc(shared_copied, 1)
            pool.wait_ge(shared_copied, 1)
            for l in range(LAYERS):
                m = shared[:, l * WC:l * WC + HID]
                pool.tensor_tensor(m, m, ident, ALU.add).then_inc(shared_ready, 1)

            def products(g, par):
                def halve(n):
                    pool.wait_ge(prod_ready, PAIRS * g + n + 1)
                    pool.tensor_tensor(EX[:, par, n, 0:2 * T], EX[:, par, n, 0:2 * T], EX[:, par, n, 2 * T:4 * T],
                                       ALU.add).then_inc(ehalf_ready, 1)

                for n in range(PAIRS):
                    pool.wait_ge(exp_ready, PAIRS * g + n + 1)
                    pool.tensor_tensor(XR[:, par, n], XR[:, par, n], EX[:, par, n], ALU.mult).then_inc(prod_ready, 1)
                    if n:
                        halve(n - 1)
                halve(PAIRS - 1)

            two_by_two(pool, 0, GROUPS, products)

            pool.wait_ge(sums_ready, GROUPS)
            pool.memset(region[96:128, 0:2 * 2 * QG * NB], 0.0).then_inc(probs_zeroed, 1)
            pool.wait_ge(probs_zeroed, 1)

            def copy_x(g, par):
                pool.wait_ge(xh_ready, g + 1)
                if not isinstance(g, int) or g >= 1:
                    pool.wait_ge(v_ready, g)
                pool.tensor_copy(XS[:], XH[:, g]).then_inc(xs_ready, 1)

            copy_x(0, 0)
            copy_x(1, 1)
            two_by_two(pool, 2, GROUPS, copy_x)

            def add_shared(g, par):
                pool.wait_ge(expert_in[par], 32 * (g - par) + 64)
                for n in range(PAIRS):
                    pool.tensor_tensor(WR[:, par, n], WR[:, par, n], shared[:], ALU.add).then_inc(expert_ready, 1)

            pool.wait_ge(shared_ready, 2)
            two_by_two(pool, 0, GROUPS, add_shared)

        @block.scalar
        def _(act):
            act.preload_act_table_set("natural_log_exp_and_others")

            def squares(cen, bank_c, sq, count):
                act.wait_ge(cen, count)
                act.activation(SQ[:], bank_c[:, 0:N], ACT.Square).then_inc(sq, 1)

            def inverse_deviation(var, bank_v, log, rstd, count):
                act.wait_ge(var, count)
                act.activation(LOGV[:], bank_v[:, 0:N], ACT.Ln, bias=eps_col[:]).then_inc(log, 1)
                act.wait_ge(log, count)
                act.activation(RSTD[:], LOGV[:], ACT.Exp, scale=-0.5).then_inc(rstd, 1)

            def pool_exp(g, par, first=False):
                for n in range(PAIRS):
                    act.wait_ge(shift_ready, PAIRS * g + n + 1)
                    if not first:
                        act.wait_ge(sums_ready, g - 1)
                    act.activation(EX[:, par, n], bank[n][:, 0:RAW], ACT.Exp).then_inc(exp_ready, 1)

            def pooling(g, par):
                squares(cen_ready, bank[4], sq_ready, g - 1)
                pool_exp(g, par)
                inverse_deviation(var_ready, bank[5], log_ready, rstd_ready, g - 1)

            pool_exp(0, 0, first=True)
            act.wait_ge(pad_shifted, 1)
            act.activation(pad_bias[:], pad_bias[:], ACT.Exp).then_inc(pad_exp, 1)
            act.wait_ge(pad_summed, 1)
            act.activation(pad_sum[:], pad_sum[:], ACT.Ln).then_inc(pad_logged, 1)
            pool_exp(1, 1, first=True)
            act.wait_ge(small_ready, 2)
            two_by_two(act, 2, GROUPS, pooling)
            for g in (GROUPS, GROUPS + 1):
                squares(cen_ready, bank[4], sq_ready, g - 1)
                inverse_deviation(var_ready, bank[5], log_ready, rstd_ready, g - 1)

            def query_rows(g, s, qg):
                act.activation(AQ[0:32, s:SLOTS:2, qg, :], bank[s][32 * qg:32 * (qg + 1), 0:N].rearrange(
                    "p (n c) -> p n c", n=PAIRS), ACT.Identity,
                    bias=bq_scaled[32 * qg:32 * (qg + 1)], scale=SCALE).then_inc(aq_ready, 1)

            def queries(g, par, s):
                act.activation(q_st[:, par, s:SLOTS:2, :], bank[s][0:64, 0:N].rearrange("p (n c) -> p n c", n=PAIRS),
                               ACT.Identity, bias=bq_scaled[:], scale=SCALE).then_inc(q_ready, 1)

            def query_evacuations(g, par):
                for i in range(6):
                    s, qg = i // 2, i % 2
                    if i < 4:
                        if i % 2 == 0:
                            act.wait_ge(qk_ready, 2 * g + s + 1)
                        query_rows(g, s, qg)
                    else:
                        queries(g, par, i - 4)
                    yield

            def attention(g, par, more=True, first=False):
                evacuations = query_evacuations(g + 1, 1 - par)
                if more:
                    act.wait_ge(mx_read, 16 * (g + 1))
                for p in range(PAIRS):
                    for i in range(4):
                        n = 4 * p + i
                        act.wait_ge(s_ready, 16 * g + n + 1)
                        if not (first and p < 2):
                            act.wait_ge(od_ready, PAIRS * g + p - 1)
                        act.activation(P[0:C, p % 2, i // 2, i % 2], bank_s[i % 2][0:C, 0:NB], ACT.Exp
                                       ).then_inc(p_ready, 1)
                        if more and n < 6:
                            next(evacuations)

            act.wait_ge(rows_in, 16 * (2 + 3 * SLOTS))
            for _ in query_evacuations(0, 0):
                pass
            act.wait_ge(probs_zeroed, 1)
            attention(0, 0, first=True)
            attention(1, 1)
            two_by_two(act, 2, GROUPS - 2, attention)
            attention(GROUPS - 2, 0)
            attention(GROUPS - 1, 1, more=False)

            def mlp(g, par, this=True, more=True):
                if this:
                    for s in range(2):
                        act.wait_ge(wi_ready, 2 * g + s + 1)
                        act.activation(R0[:, :, s], bank[3 + s][:, 0:N].rearrange("p (n c) -> p n c", n=PAIRS),
                                       ACT.Relu, bias=b_i).then_inc(r0_ready, 1)
                if more:
                    squares(cen2_ready, bank[1], sq2_ready, g + 2)
                if this:
                    for n in range(PAIRS):
                        act.wait_ge(l1_ready, 2 * g + n // 2 + 1)
                        act.activation(R1[:, n], bank[5 + n // 2][:, 2 * C * (n % 2):2 * C * (n % 2 + 1)],
                                       ACT.Relu, bias=WR[:, par, n, HID:WC]).then_inc(r1_ready, 1)
                if more:
                    inverse_deviation(var2_ready, bank[2], log2_ready, rstd2_ready, g + 2)

            mlp(-1, 1, this=False)
            two_by_two(act, 0, GROUPS - 2, mlp)
            mlp(GROUPS - 2, 0)
            mlp(GROUPS - 1, 1, more=False)

        @block.vector
        def _(dve):
            dve.memset(eps_col[:], EPS).then_inc(small_ready, 1)
            dve.wait_ge(weights_in, 48)
            dve.tensor_scalar(bq_scaled[:], b_qk[0:64], SCALE, None, ALU.mult).then_inc(small_ready, 1)

            def pool_max(g, par):
                for n in range(PAIRS):
                    dve.wait_ge(raw_ready, PAIRS * g + n + 1)
                    dve.tensor_reduce(M16[:, n], bank[n][:, 0:RAW].rearrange("p (k t) -> p t k", k=POOL), AX_X,
                                      ALU.max).then_inc(max_ready, 1)

            def pool_sums(g, par):
                dve.wait_ge(prod_ready, PAIRS * (g + 1))
                x = XR[:, par]
                dve.tensor_tensor(x[:, :, 0:2 * T], x[:, :, 0:2 * T], x[:, :, 2 * T:4 * T], ALU.add
                                  ).then_inc(xhalf_ready, 1)
                dve.wait_ge(ehalf_ready, PAIRS * (g + 1))
                e = EX[:, par]
                dve.tensor_tensor(ND[:, 1], e[:, :, 0:T], e[:, :, T:2 * T], ALU.add).then_inc(xhalf_ready, 1)
                dve.wait_ge(xhalf_ready, 2 * (g + 1))
                dve.reciprocal(RD[:], ND[:, 1]).then_inc(recip_ready, 1)
                dve.tensor_tensor(ND[:, 0], x[:, :, 0:T], x[:, :, T:2 * T], ALU.add).then_inc(sums_ready, 1)
                dve.wait_ge(recip_ready, g + 1)
                dve.wait_ge(sums_ready, g + 1)
                dve.tensor_tensor(H[:, g, :, 0:T], ND[:, 0], RD[:], ALU.mult).then_inc(h_ready, 1)

            def normalise(g):
                dve.wait_ge(rstd_ready, g + 1)
                dve.tensor_tensor(XH[:, g], bank[4][:, 0:N].rearrange("p (n c) -> p n c", n=PAIRS),
                                  RSTD[:].rearrange("p (n c) -> p n c", n=PAIRS), ALU.mult).then_inc(xh_ready, 1)

            def pooling(g, par):
                pool_max(g, par)
                pool_sums(g - 1, 1 - par)
                normalise(g - 2)

            pool_max(0, 0)
            dve.wait_ge(bias_in, 48)
            dve.tensor_reduce(pad_max[:], pad_bias[:], AX_X, ALU.max).then_inc(pad_maxed, 1)
            dve.wait_ge(pad_maxed, 1)
            dve.tensor_tensor(pad_bias[:], pad_bias[:], pad_max[:].unsqueeze(2).broadcast_to([C, HEADS, PADDED]),
                              ALU.subtract).then_inc(pad_shifted, 1)
            dve.tensor_copy(rel_q16[:], rel_q).then_inc(rel16_cast, 1)
            dve.wait_ge(pad_exp, 1)
            dve.tensor_reduce(pad_sum[:], pad_bias[:], AX_X, ALU.add).then_inc(pad_summed, 1)
            pool_max(1, 1)
            pool_sums(0, 0)
            dve.wait_ge(pad_logged, 1)
            dve.tensor_tensor(pad_lse[:], pad_sum[:], pad_max[:], ALU.add).then_inc(pad_done, 1)
            dve.wait_ge(pad_done, 1)
            dve.wait_ge(rel16_cast, 1)
            dve.tensor_copy(rel_q16[:, :, T:T + 1], pad_lse[:].unsqueeze(2)).then_inc(rel16_done, 1)
            dve.wait_ge(pad_flipped, 1)
            dve.tensor_copy(pad_rows[:], bank[6][0:HEADS, 0:C]).then_inc(pad_turned, 1)
            two_by_two(dve, 2, GROUPS, pooling)
            pool_sums(GROUPS - 1, 1)
            normalise(GROUPS - 2)
            normalise(GROUPS - 1)

            def key_evacuations(g, par):
                for s in range(2):
                    src = bank[s][:, 0:N].rearrange("p (n c) -> p n c", n=PAIRS)
                    dve.wait_ge(qk_ready, 2 * g + s + 1)
                    dve.tensor_scalar(k_st[64:128, s:SLOTS:2, :], src[64:128], b_qk[64:128], None, ALU.add
                                      ).then_inc(k16_ready, 1)
                    for qg in range(QG):
                        rows = slice(64 + 32 * qg, 96 + 32 * qg)
                        dve.tensor_scalar(A[0:32, par, s:SLOTS:2, qg, 0:K], src[rows, :, 0:K], b_qk[rows], None,
                                          ALU.add).then_inc(key_ready, 1)

            def values(g, par):
                dve.wait_ge(v_ready, g + 1)
                dve.tensor_tensor(
                    Vm[0:K, par].rearrange("p (s h e) -> p s h e", s=SLOTS, e=40)[:, :, :, 0:HD],
                    bank[2][0:K, :].rearrange("p (s h e) -> p s h e", s=SLOTS, h=HEADS),
                    b_v.rearrange("p (h e) -> p h e", h=HEADS).unsqueeze(1).broadcast_to([K, SLOTS, HEADS, HD]),
                    ALU.add).then_inc(vm_ready, 1)

            def max_item(g, par, item):
                dve.wait_ge(mx_filled, MAX_ITEMS * g + item + 1)
                src = bank_max[item % 2]
                if item in (T0_AT, MAX_ITEMS - 1):
                    half = 0 if item == T0_AT else 1
                    dve.tensor_scalar(neg_max[:, par, half], src[0:32, 0:C], -1.0, None, ALU.mult
                                      ).then_inc(negmax_ready, 1)
                else:
                    m = item - (item > T0_AT)
                    dve.tensor_reduce(mx[:, par, HH * m:HH * (m + 1)],
                                      src[0:C, 0:NB].rearrange("p (h c) -> p h c", h=HH)[:, :, 0:K], AX_X, ALU.max
                                      ).then_inc(mx_read, 1)

            def attention(g, par, more=True):
                if more:
                    key_evacuations(g + 1, 1 - par)
                max_item(g, par, MAX_ITEMS - 1)
                if more:
                    values(g + 1, 1 - par)
                item = 0
                for p in range(PAIRS):
                    for _ in range(MAX_PLAN[p] if more else 0):
                        max_item(g + 1, 1 - par, item)
                        item += 1
                    dve.wait_ge(od_ready, PAIRS * g + p + 1)
                    dve.reciprocal(RDEN[:, p % 2], OD[:, 1]).then_inc(rden_ready, 1)
                    dve.wait_ge(rden_ready, PAIRS * g + p + 1)
                    dve.tensor_tensor(XH[:, g, p], OD[:, 0], RDEN[:, p % 2], ALU.mult).then_inc(attn_ready, 1)

            dve.wait_ge(zeros_in, 64)
            dve.wait_ge(rows_in, 16 * (2 + 3 * SLOTS))
            key_evacuations(0, 0)
            values(0, 0)
            for item in range(MAX_ITEMS - 1):
                max_item(0, 0, item)
            two_by_two(dve, 0, GROUPS - 2, attention)
            attention(GROUPS - 2, 0)
            attention(GROUPS - 1, 1, more=False)

            def mlp(g, par, this=True, more=True):
                if more:
                    dve.wait_ge(proj_ready, g + 2)
                    dve.scalar_tensor_tensor(out=H[:, g + 1], in0=bank[0][:, 0:N].rearrange("p (n c) -> p n c", n=PAIRS),
                                             scalar=b_p, in1=H[:, g + 1], op0=ALU.add, op1=ALU.add
                                             ).then_inc(h2_ready, 1)
                if this:
                    for n in range(PAIRS):
                        dve.wait_ge(l2_ready, 2 * g + n // 2 + 1)
                        dve.tensor_scalar(R2[:, n].rearrange("p s c -> p (s c)"),
                                          bank[5 + n // 2][:, 2 * C * (n % 2):2 * C * (n % 2 + 1)],
                                          WR[:, par, n, WC + HID:2 * WC], 0.0, ALU.add, ALU.max
                                          ).then_inc(r2_ready, 1)
                if more:
                    dve.wait_ge(rstd2_ready, g + 2)
                    dve.tensor_tensor(X2, bank[1][:, 0:N], RSTD[:], ALU.mult).then_inc(x2_ready, 1)
                if this:
                    dve.wait_ge(wo_ready, 2 * (g + 1))
                    if not isinstance(g, int) or g >= 2:
                        dve.wait_ge(out_stored[par], 8 * (g - par))
                    dve.scalar_tensor_tensor(out=OUT[:, par], in0=bank[7][:, 0:N].rearrange("p (n c) -> p n c", n=PAIRS),
                                             scalar=b_o, in1=H[:, g], op0=ALU.add, op1=ALU.add
                                             ).then_inc(out_ready, 1)

            mlp(-1, 1, this=False)
            mlp(0, 0)
            mlp(1, 1)
            two_by_two(dve, 2, GROUPS - 2, mlp)
            mlp(GROUPS - 2, 0)
            mlp(GROUPS - 1, 1, more=False)

        @block.tensor
        def _(pe):
            def pool_raw(g, par, first=False):
                pe.wait_ge(x_in[par], 8 * (g - par) + 16)
                for n in range(PAIRS):
                    if not first:
                        pe.wait_ge(exp_ready, PAIRS * (g - 1) + n + 1)
                    pe.matmul(bank[n][:, 0:RAW], w_tok, XR[:, par, n], start=True, stop=False,
                              skip_group_check=True).then_inc(raw_ready, 1)

            def pool_shift(g, par):
                for n in range(PAIRS):
                    pe.wait_ge(max_ready, PAIRS * g + n + 1)
                    pe.matmul(bank[n][:, 0:RAW].rearrange("p (k t) -> p k t", k=POOL), neg_id[:],
                              M16[:, n].unsqueeze(1).broadcast_to([128, POOL, T]), start=False, stop=True,
                              skip_group_check=True).then_inc(shift_ready, 1)

            def centred(g, first=False):
                pe.wait_ge(h_ready, g + 1)
                if not first:
                    pe.wait_ge(xh_ready, g)
                pe.matmul(bank[4][:, 0:N], centre, H[:, g].rearrange("p n c -> p (n c)"), start=True, stop=True
                          ).then_inc(cen_ready, 1)

            def variance(g):
                pe.wait_ge(sq_ready, g + 1)
                pe.matmul(bank[5][:, 0:N], mean, SQ[:], start=True, stop=True).then_inc(var_ready, 1)

            def pooling(g, par, first=False):
                pool_raw(g, par)
                centred(g - 2, first)
                pool_shift(g, par)
                variance(g - 2)

            pe.wait_ge(weights_in, 48)
            pe.wait_ge(pads_zeroed, 1)
            pool_raw(0, 0, first=True)
            pool_shift(0, 0)
            pool_raw(1, 1)
            pool_shift(1, 1)
            pe.wait_ge(pad_done, 1)
            pe.matmul(bank[6][0:HEADS, 0:C], pad_lse[:], cst[0:C, C_FLIP:C_FLIP + C], start=True, stop=True
                      ).then_inc(pad_flipped, 1)
            pooling(2, 0, first=True)
            pooling(3, 1)
            two_by_two(pe, 4, GROUPS, pooling)
            for g in (GROUPS - 2, GROUPS - 1):
                centred(g)
                variance(g)

            def queries_keys(g, par, first=False):
                if not first:
                    pe.wait_ge(q_ready, 2 * g)
                    pe.wait_ge(key_ready, 4 * g)
                pe.wait_ge(xh_ready, g + 1)
                for s in range(2):
                    pe.matmul(bank[s][:, 0:N], w_qk[s], XH[:, g].rearrange("p n c -> p (n c)"), start=True,
                              stop=True).then_inc(qk_ready, 1)

            def values(g, par, first=False):
                pe.wait_ge(xs_ready, g + 1)
                if not first:
                    pe.wait_ge(vm_ready, g)
                for n in range(PAIRS):
                    mm = pe.matmul(bank[2][0:C, 128 * n:128 * (n + 1)], XS[:, n], w_v, start=True, stop=True)
                mm.then_inc(v_ready, 1)

            def max_item(g, par, item, first=False):
                if item == T0_AT or item == MAX_ITEMS - 1:
                    half = 0 if item == T0_AT else 1
                    pe.wait_ge(mx_read, 16 * g + (T0_AT if half == 0 else 16))
                    pe.transpose(bank_max[item % 2][0:32, 0:C], mx[:, par, 32 * half:32 * (half + 1)],
                                 ident[0:C, 0:C]).then_inc(mx_filled, 1)
                    return
                m = item - (item > T0_AT)
                if item == 0:
                    pe.wait_ge(kdiag_in, 16 * HEADS * (g + 1))
                    pe.wait_ge(aq_ready, 4 * (g + 1))
                if item in (1, T0_AT + 2) and not (first and item == 1):
                    pe.wait_ge(negmax_ready, 2 * g + (item > 1))
                elif item == 0 and not first:
                    pe.wait_ge(mx_read, 16 * g)
                elif item >= 2:
                    pe.wait_ge(mx_read, 16 * g + (m if item == T0_AT + 1 else m - 1))
                s, qg = m // 2, m % 2
                pe.matmul(bank_max[item % 2][0:C, 0:NB], AQ[:, s, qg],
                          BK[:, s, qg].rearrange("p h c -> p (h c)"), start=True, stop=True
                          ).then_inc(mx_filled, 1)

            def scores(g, par, p, i, first=False):
                n = 4 * p + i
                if n == 0:
                    pe.wait_ge(qdiag_in, 16 * HEADS * (g + 1))
                    pe.wait_ge(key_ready, 4 * (g + 1))
                if n % 8 == 0:
                    pe.wait_ge(negmax_in, 16 * (2 * g + n // 8 + 1))
                if not (first and n < 2):
                    pe.wait_ge(p_ready, 16 * g + n - 1)
                s, qg = 2 * p + i // 2, i % 2
                pe.matmul(bank_s[i % 2][0:C, 0:NB], A[0:ROWS_K + K, par, s, qg],
                          BQ[0:ROWS_K + K, par, s, qg].rearrange("p h c -> p (h c)"), start=True, stop=True
                          ).then_inc(s_ready, 1)

            def outputs(g, par, p, first=False):
                pe.wait_ge(p_ready, 16 * g + 4 * (p + 1))
                if p == 0:
                    pe.wait_ge(vm_ready, g + 1)
                if not (first and p == 0):
                    pe.wait_ge(attn_ready, PAIRS * g + p)
                for kind in range(2):
                    for hh in range(HH):
                        for s in range(2):
                            for qg in range(QG):
                                j = 2 * s + qg
                                at = (2 * p + s) * VB + qg * (VB // 2) + 32 * hh
                                lhs = Vm[:, par, at:at + 32] if kind == 0 else ones_head[hh]
                                mm = pe.matmul(OD[32 * j:32 * (j + 1), kind], lhs,
                                               P[:, p % 2, s, qg, C * hh:C * (hh + 1)], start=(hh == 0),
                                               stop=(hh == HH - 1))
                mm.then_inc(od_ready, 1)

            def attention(g, par, more=True, first=False):
                if more:
                    queries_keys(g + 1, 1 - par)
                item = 0
                for p in range(PAIRS):
                    planned = MAX_PLAN[p] if more else 0
                    for i in range(4):
                        scores(g, par, p, i, first)
                        if p > 0 and planned:
                            max_item(g + 1, 1 - par, item)
                            item += 1
                            planned -= 1
                    if p == 0:
                        max_item(g, par, MAX_ITEMS - 1)
                        if more:
                            values(g + 1, 1 - par)
                    outputs(g, par, p, first)
                    for _ in range(planned):
                        max_item(g + 1, 1 - par, item)
                        item += 1

            pe.wait_ge(xh_ready, GROUPS)
            queries_keys(0, 0, first=True)
            values(0, 0, first=True)
            pe.wait_ge(rows_in, 16 * (2 + 3 * SLOTS))
            pe.wait_ge(zeros_in, 64)
            for item in range(MAX_ITEMS - 1):
                max_item(0, 0, item, first=True)
            pe.wait_ge(probs_zeroed, 1)
            attention(0, 0, first=True)
            attention(1, 1)
            two_by_two(pe, 2, GROUPS - 2, attention)
            attention(GROUPS - 2, 0)
            attention(GROUPS - 1, 1, more=False)

            def layer(g, par, l, done, came, R):
                for half in range(2):
                    if l == 0:
                        if half == 0:
                            pe.wait_ge(came, 2 * (g + 1))
                        pe.wait_ge(expert_ready, PAIRS * g + 2 * half + 2)
                        if not isinstance(g, int) or g >= 1:
                            pe.wait_ge(r2_ready, PAIRS * (g - 1) + 2 * half + 2)
                    else:
                        pe.wait_ge(came, PAIRS * g + 2 * half + 2)
                    for n in (2 * half, 2 * half + 1):
                        mm = pe.matmul(bank[5 + half][:, 2 * C * (n % 2):2 * C * (n % 2 + 1)],
                                       WR[:, par, n, l * WC:l * WC + HID], R[:, n].rearrange("p s c -> p (s c)"),
                                       start=True, stop=True)
                    mm.then_inc(done, 1)

            def mlp(g, par, this=True, more=True, first=False):
                if this:
                    pe.wait_ge(x2_ready, g + 1)
                    for s in range(2):
                        pe.matmul(bank[3 + s][:, 0:N], w_i[s], X2, start=True, stop=True).then_inc(wi_ready, 1)
                if more:
                    pe.wait_ge(attn_ready, PAIRS * (g + 2))
                    pe.matmul(bank[0][:, 0:N], w_p, XH[:, g + 1].rearrange("p n c -> p (n c)"), start=True,
                              stop=True).then_inc(proj_ready, 1)
                if this:
                    layer(g, par, 0, l1_ready, r0_ready, R0)
                if more:
                    pe.wait_ge(h2_ready, g + 2)
                    pe.matmul(bank[1][:, 0:N], centre, H[:, g + 1].rearrange("p n c -> p (n c)"), start=True,
                              stop=True).then_inc(cen2_ready, 1)
                if this:
                    layer(g, par, 1, l2_ready, r1_ready, R1)
                if more:
                    pe.wait_ge(sq2_ready, g + 2)
                    pe.matmul(bank[2][:, 0:N], mean, SQ[:], start=True, stop=True).then_inc(var2_ready, 1)
                if this:
                    pe.wait_ge(r2_ready, PAIRS * (g + 1))
                    if not first:
                        pe.wait_ge(out_ready, g)
                    for s in range(2):
                        pe.matmul(bank[7][64 * s:64 * (s + 1), 0:N].rearrange("p (n c) -> p n c", n=PAIRS), w_o,
                                  R2[:, :, s], start=True, stop=True).then_inc(wo_ready, 1)

            pe.wait_ge(attn_ready, PAIRS * GROUPS)
            mlp(-1, 1, this=False)
            mlp(0, 0, first=True)
            mlp(1, 1)
            two_by_two(pe, 2, GROUPS - 2, mlp)
            mlp(GROUPS - 2, 0)
            mlp(GROUPS - 1, 1, more=False)


MAX_PLAN = (0, 6, 6, 5)


def prepared(inputs):
    f32 = np.float32
    x = np.asarray(inputs["x"])[:, :RAW].reshape(GROUPS, PAIRS, 2, T, POOL, D)
    xT = np.ascontiguousarray(x.transpose(0, 2, 5, 1, 4, 3)).reshape(GROUPS, 128, PAIRS, RAW)
    qkv, bqkv = np.asarray(inputs["L0_attn_qkv_weight"]), np.asarray(inputs["L0_attn_qkv_bias"])
    w = np.zeros((128, W_ALL), f32)
    for s in range(2):
        rows = slice(64 * s, 64 * (s + 1))
        w[rows, W_TOK + 64 * s:W_TOK + 64 * (s + 1)] = inputs["L0_tok_W"]
        w[rows, W_QK + 128 * s:W_QK + 128 * (s + 1)] = qkv[0:128].T
        w[rows, W_V + 64 * s:W_V + 64 * (s + 1)] = qkv[128:192].T
        w[rows, W_P + 64 * s:W_P + 64 * (s + 1)] = np.asarray(inputs["L0_attn_proj_weight"]).T
        w[rows, W_I + 128 * s:W_I + 128 * (s + 1)] = np.asarray(inputs["L0_ffn_Wi"]).T
        w[rows, W_BIAS + 1] = inputs["L0_attn_proj_bias"]
        w[rows, W_BIAS + 3] = inputs["L0_ffn_bo"]
    w[:, W_O:W_O + D] = np.asarray(inputs["L0_ffn_Wo"]).T
    for l in range(LAYERS):
        w[:, W_S + l * WC:W_S + l * WC + HID] = np.asarray(inputs["L0_ffn_Ws"])[l, 0].T
        w[:, W_S + l * WC + HID] = np.asarray(inputs["L0_ffn_bs"])[l, 0]
    w[:, W_BIAS] = bqkv[0:128]
    w[:, W_BIAS + 2] = inputs["L0_ffn_bi"]
    w[:, W_BV:W_BV + D] = bqkv[None, 128:192]
    wr, br = np.asarray(inputs["L0_ffn_Wr"]), np.asarray(inputs["L0_ffn_br"])
    experts = np.concatenate([wr.transpose(1, 3, 0, 2), br.transpose(1, 2, 0)[..., None]], axis=3)
    experts = np.ascontiguousarray(experts).reshape(wr.shape[1], 128, LAYERS * WC)
    tab = np.ascontiguousarray(np.asarray(inputs["L0_attn_bias_table"]).T)

    half = np.kron(np.eye(2, dtype=f32), np.full((D, D), 1.0 / D, f32))
    c = np.zeros((128, C_ALL), f32)
    c[:, C_CEN:C_CEN + 128] = np.eye(128, dtype=f32) - half
    c[:, C_MEAN:C_MEAN + 128] = half
    c[:, C_ID:C_ID + 128] = np.eye(128, dtype=f32)
    for hh in range(HH):
        c[0:K, C_ONES + 40 * hh:C_ONES + 40 * hh + HD] = 1.0
    c[0:C, C_FLIP:C_FLIP + C] = np.eye(C)[::-1]
    id16 = np.zeros((128, 128 + C), mybir.dt.np(BF16))
    id16[:, 0:128] = -np.eye(128)
    id16[0:C, 128:128 + C] = np.eye(C)[::-1]
    key_rows = np.zeros((K + 1, C), f32)
    key_rows[0, 0:K] = 1.0
    key_rows[1:K, 0:T] = np.eye(T)[::-1]
    key_rows[K, T] = 1.0
    return {"xT": xT, "weights": w, "consts": c, "id16": id16, "key_rows": key_rows,
            "zeros": np.zeros((1, 2 * SLOTS * QG * NB), f32), "tab": tab, "tab_rev": np.ascontiguousarray(tab[:, ::-1]),
            "experts": experts, "route": np.asarray(inputs["L0_ffn_route_id"]).reshape(1, -1)}


def kernel(**inputs):
    import concourse.bacc as bacc
    from concourse.bass_utils import run_bass_kernel_spmd

    nc = bacc.Bacc("TRN2", target_bir_lowering=False, num_devices=1)
    arrays = prepared(inputs)
    args = [nc.dram_tensor(f"in_{k}", a.shape, mybir.dt.from_np(a.dtype), kind="ExternalInput").ap()
            for k, a in arrays.items()]
    args.append(nc.dram_tensor("outT", (GROUPS, 128, PAIRS, T), F32, kind="ExternalOutput").ap())
    build(nc, *args)
    r = run_bass_kernel_spmd(nc, [{f"in_{k}": a for k, a in arrays.items()}], core_ids=[0])
    out = np.asarray(r.results[0]["outT"]).reshape(GROUPS, 2, D, PAIRS, T)
    return np.ascontiguousarray(out.transpose(0, 3, 1, 4, 2)).reshape(B, T, D)
```

```python
from contextlib import ExitStack

import numpy as np

import concourse.bass as bass
from concourse import mybir

F32 = mybir.dt.float32
BF16 = mybir.dt.bfloat16
I32 = mybir.dt.int32
ACT = mybir.ActivationFunctionType
ALU = mybir.AluOpType
AX_X = mybir.AxisListType.X

B, D = 128, 64
POOL = 4
T = 375 // POOL
WINDOW = 128
PADDED = WINDOW - T
C = T + 1
HEADS, HD = 8, 8
HH, QG = 4, 2
HID, LAYERS = 128, 2
PAIRS = 4
SLOTS = 2 * PAIRS
GROUPS = B // SLOTS
RAW = POOL * T
N = PAIRS * C
NB = HH * C
NT = 2 * WINDOW - 1
WC = HID + 1
ROWS_Q = 32
ROWS_K = 33
VB = QG * HH * 40
SCALE = HD ** -0.5
EPS = 1e-5

W_TOK, W_QK, W_V, W_P, W_I, W_O = 0, 128, 384, 512, 640, 896
W_S = 960
W_BIAS = W_S + LAYERS * WC
W_BV = W_BIAS + 4
W_ALL = W_BV + D
C_CEN, C_MEAN, C_ID, C_ONES, C_FLIP, C_ALL = 0, 128, 256, 384, 512, 512 + C


FIRST, LAST = -3, GROUPS + 1
STEADY = (2, GROUPS - 4)


def steps(eng, step):
    for t in range(FIRST, STEADY[0]):
        step(t, t % 2)
    with eng.Fori(STEADY[0] // 2, STEADY[1] // 2) as i:
        for par in range(2):
            step(2 * i + par, par)
    for t in range(STEADY[1], LAST + 1):
        step(t, t % 2)


def there(group):
    return not isinstance(group, int) or 0 <= group < GROUPS


def after_first(group):
    return not isinstance(group, int) or 0 < group < GROUPS


def build(nc, xT, weights, consts, id16, key_rows, tab, tab_rev, experts, route, outT):
    with ExitStack() as ctx:
        def sb(name, shape, dt=F32):
            return ctx.enter_context(nc.sbuf_tensor(name, shape, dt))

        def sem(name):
            return ctx.enter_context(nc.semaphore(name))

        bank = [ctx.enter_context(nc.psum_tensor(f"bank{i}", [128, 512], F32)) for i in range(8)]

        wts = sb("wts", [128, W_ALL])
        cst = sb("cst", [128, C_ALL])
        neg_id = sb("neg_id", [128, 128], BF16)
        route_sb = sb("route_sb", [1, B // 2], I32)
        bq_scaled = sb("bq_scaled", [64, 1])
        eps_col = sb("eps_col", [128, 1])
        shared = sb("shared", [128, LAYERS * WC])
        rel_q16 = sb("rel_q16", [C, HEADS, C], BF16)
        pad_bias = sb("pad_bias", [C, HEADS, PADDED])
        pad_max = sb("pad_max", [C, HEADS])
        pad_sum = sb("pad_sum", [C, HEADS])
        pad_lse = sb("pad_lse", [C, HEADS])
        pad_rows = sb("pad_rows", [HEADS, C])

        H = sb("H", [128, GROUPS, PAIRS, C])
        XN = sb("XN", [128, PAIRS, C])
        AO = sb("AO", [128, 2, PAIRS, C])
        NORM1, NORM2 = sb("NORM1", [128, N]), sb("NORM2", [128, N])

        A = sb("A", [128, 2, SLOTS, QG, C])
        BQ = sb("BQ", [128, 2, SLOTS, QG, HH, C])
        AQ = sb("AQ", [128, SLOTS, QG, C], BF16)
        BK = sb("BK", [128, SLOTS, QG, HH, C], BF16)
        staging = sb("staging", [128, 2, SLOTS * C])
        q_st = staging[0:64].rearrange("p g (s c) -> p g s c", s=SLOTS)
        rel_q = staging[0:C, 0].rearrange("p (h c) -> p h c", h=HEADS)
        rel_k = staging[0:C, 1].rearrange("p (h c) -> p h c", h=HEADS)
        k_st = sb("k_st", [128, SLOTS, C], BF16)
        Vm = sb("Vm", [128, 2, SLOTS * VB])
        P = sb("P", [128, 2, 2, QG, NB])
        mx = sb("mx", [C, 2, SLOTS * HEADS])
        neg_max = sb("neg_max", [32, 2, 2, C])
        RDEN = sb("RDEN", [128, 2, C])

        XR = sb("XR", [128, 2, PAIRS, RAW])
        EX = sb("EX", [128, PAIRS, RAW])
        M16 = sb("M16", [128, PAIRS, T], BF16)
        ND = sb("ND", [128, 2, PAIRS, T])
        RD = sb("RD", [128, PAIRS, T])

        WR = sb("WR", [128, 2, PAIRS, LAYERS * WC])
        R0, R1, R2 = (sb(f"R{i}", [128, PAIRS, 2, C]) for i in range(3))
        X2 = sb("X2", [128, N])

        token_weights_in, weights_in, route_in, bias_in = (
            sem("token_weights_in"), sem("weights_in"), sem("route_in"), sem("bias_in"))
        pad_maxed, pad_shifted, pad_exp, pad_summed, pad_logged, pad_done = (
            sem("pad_maxed"), sem("pad_shifted"), sem("pad_exp"), sem("pad_summed"), sem("pad_logged"),
            sem("pad_done"))
        rel16_cast, rel16_done = sem("rel16_cast"), sem("rel16_done")
        pad_flipped, pad_turned, pad_row_in = sem("pad_flipped"), sem("pad_turned"), sem("pad_row_in")
        max_rows_in, rows_in, small_ready = sem("max_rows_in"), [sem("rows_in0"), sem("rows_in1")], sem("small_ready")
        shared_copied, shared_ready = sem("shared_copied"), sem("shared_ready")
        pads_zeroed, probs_zeroed, bk_zeroed, vm_zeroed, bq_zeroed = (
            sem("pads_zeroed"), sem("probs_zeroed"), sem("bk_zeroed"), sem("vm_zeroed"), [sem("bq_zeroed0"), sem("bq_zeroed1")])
        x_in = [sem("x_in0"), sem("x_in1")]
        raw_ready, max_ready, shift_ready = sem("raw_ready"), sem("max_ready"), sem("shift_ready")
        exp_ready, prod_ready = sem("exp_ready"), sem("prod_ready")
        half_ready, sums_ready, recip_ready, h_ready = (
            sem("half_ready"), sem("sums_ready"), sem("recip_ready"), sem("h_ready"))
        cen_ready, sq_ready, var_ready, log_ready, rstd_ready, xn_ready = (
            sem("cen_ready"), sem("sq_ready"), sem("var_ready"), sem("log_ready"), sem("rstd_ready"), sem("xn_ready"))
        qk_ready, v_ready, vm_ready = sem("qk_ready"), sem("v_ready"), sem("vm_ready")
        k16_ready, aq_ready, q_ready, key_ready = sem("k16_ready"), sem("aq_ready"), sem("q_ready"), sem("key_ready")
        kdiag_in, qdiag_in, negmax_in = sem("kdiag_in"), sem("qdiag_in"), sem("negmax_in")
        mx_filled, mx_read = sem("mx_filled"), sem("mx_read")
        s_ready, p_ready, od_ready, rden_ready, attn_ready = (
            sem("s_ready"), sem("p_ready"), sem("od_ready"), sem("rden_ready"), sem("attn_ready"))
        expert_in, expert_ready = [sem("expert_in0"), sem("expert_in1")], sem("expert_ready")
        proj_ready, h2_ready, cen2_ready, sq2_ready, var2_ready, log2_ready, rstd2_ready, x2_ready = (
            sem("proj_ready"), sem("h2_ready"), sem("cen2_ready"), sem("sq2_ready"), sem("var2_ready"),
            sem("log2_ready"), sem("rstd2_ready"), sem("x2_ready"))
        wi_ready, r0_ready, l1_ready, r1_ready, l2_ready, r2_ready = (
            sem("wi_ready"), sem("r0_ready"), sem("l1_ready"), sem("r1_ready"), sem("l2_ready"), sem("r2_ready"))
        wo_ready, out_ready, out_stored = sem("wo_ready"), sem("out_ready"), sem("out_stored")

        block = ctx.enter_context(nc.Block())
        w_tok, w_v, w_p = wts[:, W_TOK:W_TOK + 128], wts[:, W_V:W_V + 128], wts[:, W_P:W_P + 128]
        w_qk = [wts[:, W_QK + 128 * s:W_QK + 128 * (s + 1)] for s in range(2)]
        w_i = [wts[:, W_I + 128 * s:W_I + 128 * (s + 1)] for s in range(2)]
        w_o = wts[:, W_O:W_O + D]
        b_qk, b_p, b_i, b_o = (wts[:, W_BIAS + i:W_BIAS + i + 1] for i in range(4))
        b_v = wts[0:C, W_BV:W_BV + D]
        centre, mean, ident = cst[:, C_CEN:C_CEN + 128], cst[:, C_MEAN:C_MEAN + 128], cst[:, C_ID:C_ID + 128]
        ones_head = [cst[:, C_ONES + 32 * hh:C_ONES + 32 * (hh + 1)] for hh in range(HH)]

        bank_s = [bank[5], bank[6]]
        OD = bank[7][:, 0:2 * C].rearrange("p (k c) -> p k c", k=2)

        def by_pair(ap):
            return ap.rearrange("p (n c) -> p n c", n=PAIRS)

        ITEMS, T0_AT = 4 * PAIRS + 2, 10

        def max_bank(g, item):
            return bank_s[0] if isinstance(g, int) and g == 0 and item % 2 and item < ITEMS - 1 else bank[3]

        @block.sync
        def _(sp):
            sp.dma_start(wts[:, W_TOK:W_QK], weights[:, W_TOK:W_QK]).then_inc(token_weights_in, 16)
            sp.dma_start(XR[:, 0], xT[0]).then_inc(x_in[0], 16)
            sp.dma_start(neg_id[:], id16[:, 0:128]).then_inc(token_weights_in, 16)
            sp.dma_start(wts[:, W_QK:W_ALL], weights[:, W_QK:W_ALL]).then_inc(weights_in, 16)
            sp.dma_start(cst[:], consts).then_inc(weights_in, 16)
            sp.dma_start(pad_bias[:], bass.AP(tab_rev.tensor, WINDOW - C + T, [[1, C], [NT, HEADS], [1, PADDED]])
                         ).then_inc(bias_in, 16)
            sp.dma_start(rel_q, bass.AP(tab_rev.tensor, WINDOW - C, [[1, C], [NT, HEADS], [1, C]])
                         ).then_inc(bias_in, 16)
            sp.dma_start(rel_k[0:T], bass.AP(tab.tensor, WINDOW - T, [[1, T], [NT, HEADS], [1, C]])
                         ).then_inc(bias_in, 16)
            sp.dma_start(route_sb[:], route).then_inc(route_in, 16)

            sp.dma_start(AQ[ROWS_Q:ROWS_Q + C].rearrange("p s g c -> p (s g) c"),
                         bass.AP(id16.tensor, 128, [[128 + C, C], [0, SLOTS * QG], [1, C]])).then_inc(max_rows_in, 16)

            def operand_rows(par):
                sp.dma_start(A[32:33 + C, par].rearrange("p s g c -> p (s g) c"),
                             bass.AP(key_rows.tensor, 0, [[C, C + 1], [0, SLOTS * QG], [1, C]])
                             ).then_inc(rows_in[par], 16)
                for s in range(SLOTS):
                    sp.dma_start(BQ[ROWS_K:ROWS_K + C, par, s].rearrange("p g h c -> p (g h) c"), rel_k
                                 ).then_inc(rows_in[par], 16)

            def bias_rows():
                sp.wait_ge(pad_turned, 1)
                sp.dma_start(rel_k[T:C], pad_rows[:]).then_inc(pad_row_in, 16)
                sp.wait_ge(rel16_done, 1)
                for s in range(SLOTS):
                    sp.dma_start(BK[ROWS_Q:ROWS_Q + C, s].rearrange("p g h c -> p (g h) c"), rel_q16[:]
                                 ).then_inc(max_rows_in, 16)
                sp.wait_ge(pad_row_in, 16)
                sp.wait_ge(bias_in, 48)
                operand_rows(0)

            def key_diagonals(g):
                sp.wait_ge(k16_ready, 2 * (g + 1))
                for h in range(HEADS):
                    hh, qg = h % HH, h // HH
                    sp.dma_start(BK[HD * hh:HD * (hh + 1), :, qg, hh, :], k_st[64 + HD * h:64 + HD * (h + 1)]
                                 ).then_inc(kdiag_in, 16)

            def query_diagonals(g, par):
                sp.wait_ge(q_ready, 2 * (g + 1))
                for h in range(HEADS):
                    hh, qg = h % HH, h // HH
                    sp.dma_start(BQ[HD * hh:HD * (hh + 1), par, :, qg, hh, :], q_st[HD * h:HD * (h + 1), par]
                                 ).then_inc(qdiag_in, 16)

            def negmax(g, par, half):
                sp.wait_ge(mx_read, ITEMS * g + (ITEMS if half else T0_AT + 1))
                sp.dma_start(BQ[32:33, par, 4 * half:4 * (half + 1)].rearrange("o s g h c -> o (s g h) c"),
                             neg_max[:, par, half]).then_inc(negmax_in, 16)

            def step(t, par):
                if there(t + 1):
                    key_diagonals(t + 1)
                if there(t):
                    negmax(t, par, 1)
                if there(t - 2):
                    sp.wait_ge(out_ready, t - 1)
                    sp.dma_start(outT[t - 2], H[:, t - 2, :, 0:T]).then_inc(out_stored, 16)
                if there(t):
                    if there(t - 2):
                        sp.wait_ge(r2_ready, PAIRS * (t - 1))
                    for n in range(PAIRS):
                        r = sp.value_load(route_sb[0:1, bass.ds(PAIRS * t + n, 1)], min_val=0, max_val=15)
                        sp.dma_start(WR[:, par, n], experts[r]).then_inc(expert_in[par], 16)
                if there(t + 1):
                    query_diagonals(t + 1, 1 - par)
                    if isinstance(t, int) and t == -1:
                        operand_rows(1)
                    negmax(t + 1, 1 - par, 0)
                if there(t + 4):
                    if there(t + 2):
                        sp.wait_ge(sums_ready, 2 * (t + 3))
                    sp.dma_start(XR[:, par], xT[t + 4]).then_inc(x_in[par], 16)
                if isinstance(t, int) and t == FIRST:
                    bias_rows()
                    sp.wait_ge(route_in, 16)
                    sp.wait_ge(bk_zeroed, 1)
                    sp.wait_ge(bq_zeroed[0], 1)
                if isinstance(t, int) and t == -1:
                    sp.wait_ge(bq_zeroed[1], 1)

            steps(sp, step)
            sp.wait_ge(out_stored, 16 * GROUPS)

        @block.gpsimd
        def _(pool):
            pool.memset(H[:, :, :, T:C], 0.0).then_inc(pads_zeroed, 1)
            pool.wait_ge(pads_zeroed, 1)
            pool.memset(BK[0:32].bitcast(F32), 0.0).then_inc(bk_zeroed, 1)
            pool.wait_ge(bk_zeroed, 1)
            pool.memset(P[64:128], 0.0).then_inc(probs_zeroed, 1)
            pool.wait_ge(probs_zeroed, 1)

            def products(g, par):
                def halve(n):
                    pool.wait_ge(prod_ready, PAIRS * g + n + 1)
                    for summed in (EX[:, n], XR[:, par, n]):
                        pool.tensor_tensor(summed[:, 0:2 * T], summed[:, 0:2 * T], summed[:, 2 * T:4 * T], ALU.add
                                           ).then_inc(half_ready, 1)

                for n in range(PAIRS):
                    pool.wait_ge(exp_ready, PAIRS * g + n + 1)
                    pool.tensor_tensor(XR[:, par, n], XR[:, par, n], EX[:, n], ALU.mult).then_inc(prod_ready, 1)
                    if n:
                        halve(n - 1)
                halve(PAIRS - 1)

            def add_shared(g, par):
                pool.wait_ge(expert_in[par], 32 * (g - par) + 64)
                for n in range(PAIRS):
                    pool.tensor_tensor(WR[:, par, n], WR[:, par, n], shared[:], ALU.add).then_inc(expert_ready, 1)

            def step(t, par):
                if there(t + 3):
                    products(t + 3, 1 - par)
                if there(t):
                    add_shared(t, par)
                if isinstance(t, int) and t == FIRST:
                    pool.wait_ge(weights_in, 32)
                    pool.tensor_copy(shared[:], wts[:, W_S:W_S + LAYERS * WC]).then_inc(shared_copied, 1)
                    pool.wait_ge(shared_copied, 1)
                    for l in range(LAYERS):
                        m = shared[:, l * WC:l * WC + HID]
                        pool.tensor_tensor(m, m, ident, ALU.add).then_inc(shared_ready, 1)
                    pool.wait_ge(shared_ready, 2)
                    pool.memset(Vm[:], 0.0).then_inc(vm_zeroed, 1)
                    pool.wait_ge(vm_zeroed, 1)
                if isinstance(t, int) and t == FIRST + 1:
                    pool.memset(BQ[0:32, 1], 0.0).then_inc(bq_zeroed[1], 1)
                    pool.wait_ge(bq_zeroed[1], 1)

            steps(pool, step)

        @block.scalar
        def _(act):
            act.preload_act_table_set("natural_log_exp_and_others")

            def squares(cen, bank_c, norm, sq, g):
                act.wait_ge(cen, g + 1)
                act.activation(norm[:], bank_c[:, 0:N], ACT.Square).then_inc(sq, 1)

            def inverse_deviation(var, bank_v, norm, log, rstd, g):
                act.wait_ge(var, g + 1)
                act.activation(norm[:], bank_v[:, 0:N], ACT.Ln, bias=eps_col[:]).then_inc(log, 1)
                act.wait_ge(log, g + 1)
                act.activation(norm[:], norm[:], ACT.Exp, scale=-0.5).then_inc(rstd, 1)

            def pool_exp(g, n):
                act.wait_ge(shift_ready, PAIRS * g + n + 1)
                if after_first(g):
                    act.wait_ge(sums_ready, 2 * g)
                act.activation(EX[:, n], bank[n % 2][:, 0:RAW], ACT.Exp).then_inc(exp_ready, 1)

            def padded_keys():
                act.wait_ge(pad_shifted, 1)
                act.activation(pad_bias[:], pad_bias[:], ACT.Exp).then_inc(pad_exp, 1)
                act.wait_ge(pad_summed, 1)
                act.activation(pad_sum[:], pad_sum[:], ACT.Ln).then_inc(pad_logged, 1)

            def queries(g, par, i):
                if i < 4:
                    s, qg = i // 2, i % 2
                    act.wait_ge(qk_ready, 2 * g + s + 1)
                    if i == 0 and after_first(g):
                        act.wait_ge(mx_read, ITEMS * g - 1)
                    act.activation(AQ[0:32, s:SLOTS:2, qg, :], by_pair(bank[s][32 * qg:32 * (qg + 1), 0:N]),
                                   ACT.Identity, bias=bq_scaled[32 * qg:32 * (qg + 1)], scale=SCALE
                                   ).then_inc(aq_ready, 1)
                else:
                    s = i - 4
                    act.activation(q_st[:, par, s:SLOTS:2, :], by_pair(bank[s][0:64, 0:N]), ACT.Identity,
                                   bias=bq_scaled[:], scale=SCALE).then_inc(q_ready, 1)

            def keys(g, par):
                for s in range(2):
                    act.wait_ge(k16_ready, 2 * g + s + 1)
                    for qg in range(QG):
                        rows = slice(64 + 32 * qg, 96 + 32 * qg)
                        act.activation(A[0:32, par, s:SLOTS:2, qg, :], by_pair(bank[s][rows, 0:N]),
                                       ACT.Identity, bias=b_qk[rows]).then_inc(key_ready, 1)

            def exps(t, p, which):
                for i in which:
                    if there(t):
                        act.wait_ge(s_ready, 16 * t + 4 * p + i + 1)
                        if p >= 2 or after_first(t):
                            act.wait_ge(od_ready, PAIRS * t + p - 1)
                        act.activation(P[0:C, p % 2, i // 2, i % 2], bank_s[i % 2][0:C, 0:NB], ACT.Exp
                                       ).then_inc(p_ready, 1)

            def step(t, par):
                for i in range(4):
                    exps(t, 0, (i,))
                    if there(t + 1):
                        for evac in ((), (0, 1), (2, 3), ())[i]:
                            queries(t + 1, 1 - par, evac)
                if there(t - 2):
                    for n in range(PAIRS):
                        act.wait_ge(l2_ready, 2 * (t - 2) + n // 2 + 1)
                        act.activation(R2[:, n].rearrange("p s c -> p (s c)"),
                                       bank[2 + 2 * (n // 2)][:, 2 * C * (n % 2):2 * C * (n % 2 + 1)],
                                       ACT.Relu, bias=WR[:, par, n, WC + HID:2 * WC]).then_inc(r2_ready, 1)
                if there(t + 1):
                    queries(t + 1, 1 - par, 4)
                    queries(t + 1, 1 - par, 5)
                    keys(t + 1, 1 - par)

                exps(t, 1, range(4))
                if there(t + 3):
                    pool_exp(t + 3, 0)
                    pool_exp(t + 3, 1)
                if there(t - 1):
                    squares(cen2_ready, bank[4], NORM2, sq2_ready, t - 1)

                exps(t, 2, range(2))
                if there(t + 2):
                    squares(cen_ready, bank[0], NORM1, sq_ready, t + 2)
                exps(t, 2, range(2, 4))
                if there(t - 1):
                    inverse_deviation(var2_ready, bank[2], NORM2, log2_ready, rstd2_ready, t - 1)
                if there(t + 2):
                    inverse_deviation(var_ready, bank[1], NORM1, log_ready, rstd_ready, t + 2)
                if there(t - 1):
                    for s in range(2):
                        act.wait_ge(wi_ready, 2 * (t - 1) + s + 1)
                        act.activation(R0[:, :, s], by_pair(bank[2 + 2 * s][:, 0:N]), ACT.Relu, bias=b_i
                                       ).then_inc(r0_ready, 1)

                exps(t, 3, range(4))
                if there(t - 1):
                    for n in range(PAIRS):
                        act.wait_ge(l1_ready, 2 * (t - 1) + n // 2 + 1)
                        act.activation(R1[:, n].rearrange("p s c -> p (s c)"),
                                       bank[2 + 2 * (n // 2)][:, 2 * C * (n % 2):2 * C * (n % 2 + 1)],
                                       ACT.Relu, bias=WR[:, 1 - par, n, HID:WC]).then_inc(r1_ready, 1)
                if there(t + 3):
                    pool_exp(t + 3, 2)
                    pool_exp(t + 3, 3)
                if isinstance(t, int) and t == FIRST:
                    padded_keys()
                if isinstance(t, int) and t == -2:
                    act.wait_ge(small_ready, 2)
                    act.wait_ge(rel16_cast, 1)
                    act.wait_ge(probs_zeroed, 1)
                if isinstance(t, int) and t == -1:
                    for par in range(2):
                        act.wait_ge(rows_in[par], 16 * (1 + SLOTS))

            steps(act, step)

        @block.vector
        def _(dve):
            def setup():
                dve.memset(eps_col[:], EPS).then_inc(small_ready, 1)
                dve.memset(BQ[0:32, 0], 0.0).then_inc(bq_zeroed[0], 1)

            def padded_keys():
                dve.wait_ge(weights_in, 32)
                dve.tensor_scalar(bq_scaled[:], b_qk[0:64], SCALE, None, ALU.mult).then_inc(small_ready, 1)
                dve.wait_ge(bias_in, 48)
                dve.tensor_reduce(pad_max[:], pad_bias[:], AX_X, ALU.max).then_inc(pad_maxed, 1)
                dve.wait_ge(pad_maxed, 1)
                dve.tensor_tensor(pad_bias[:], pad_bias[:], pad_max[:].unsqueeze(2).broadcast_to([C, HEADS, PADDED]),
                                  ALU.subtract).then_inc(pad_shifted, 1)
                dve.tensor_copy(rel_q16[:], rel_q).then_inc(rel16_cast, 1)
                dve.wait_ge(pad_exp, 1)
                dve.tensor_reduce(pad_sum[:], pad_bias[:], AX_X, ALU.add).then_inc(pad_summed, 1)
                dve.wait_ge(pad_logged, 1)
                dve.tensor_tensor(pad_lse[:], pad_sum[:], pad_max[:], ALU.add).then_inc(pad_done, 1)
                dve.wait_ge(pad_done, 1)
                dve.wait_ge(rel16_cast, 1)
                dve.tensor_copy(rel_q16[:, :, T:T + 1], pad_lse[:].unsqueeze(2)).then_inc(rel16_done, 1)

            def pool_max(g, n):
                dve.wait_ge(raw_ready, PAIRS * g + n + 1)
                dve.tensor_reduce(M16[:, n], bank[n % 2][:, 0:RAW].rearrange("p (k t) -> p t k", k=POOL), AX_X,
                                  ALU.max).then_inc(max_ready, 1)

            def pool_sums(g, par):
                dve.wait_ge(half_ready, 2 * PAIRS * (g + 1))
                dve.tensor_tensor(ND[:, 1], EX[:, :, 0:T], EX[:, :, T:2 * T], ALU.add).then_inc(sums_ready, 1)
                dve.tensor_tensor(ND[:, 0], XR[:, par, :, 0:T], XR[:, par, :, T:2 * T], ALU.add
                                  ).then_inc(sums_ready, 1)
                dve.wait_ge(sums_ready, 2 * (g + 1))

            def pool_reciprocal(pairs):
                dve.reciprocal(RD[:, pairs], ND[:, 1, pairs]).then_inc(recip_ready, 1)

            def pool_ratio(g):
                dve.wait_ge(recip_ready, 3 * (g + 1))
                dve.tensor_tensor(H[:, g, :, 0:T], ND[:, 0], RD[:], ALU.mult).then_inc(h_ready, 1)

            def keys16(g):
                for s in range(2):
                    dve.wait_ge(qk_ready, 2 * g + s + 1)
                    dve.tensor_scalar(k_st[64:128, s:SLOTS:2, :], by_pair(bank[s][:, 0:N])[64:128], b_qk[64:128], None,
                                      ALU.add).then_inc(k16_ready, 1)

            def values(g, par):
                if isinstance(g, int) and g == 0:
                    dve.wait_ge(vm_zeroed, 1)
                dve.wait_ge(v_ready, g + 1)
                dve.tensor_tensor(
                    Vm[0:C, par].rearrange("p (s h e) -> p s h e", s=SLOTS, e=40)[:, :, :, 0:HD],
                    bank[2][0:C, :].rearrange("p (s h e) -> p s h e", s=SLOTS, h=HEADS),
                    b_v.rearrange("p (h e) -> p h e", h=HEADS).unsqueeze(1).broadcast_to([C, SLOTS, HEADS, HD]),
                    ALU.add).then_inc(vm_ready, 1)

            def max_item(g, par, item):
                bank_max = max_bank(g, item)
                dve.wait_ge(mx_filled, ITEMS * g + item + 1)
                if item in (T0_AT, ITEMS - 1):
                    dve.tensor_scalar(neg_max[:, par, int(item > T0_AT)], bank_max[0:32, 0:C], -1.0, None, ALU.mult
                                      ).then_inc(mx_read, 1)
                else:
                    m = item - (item > T0_AT)
                    dve.tensor_reduce(mx[:, par, HH * m:HH * (m + 1)],
                                      bank_max[0:C, 0:NB].rearrange("p (h c) -> p h c", h=HH)[:, :, 0:C], AX_X,
                                      ALU.max).then_inc(mx_read, 1)

            def divide(g, par, p):
                dve.wait_ge(od_ready, PAIRS * g + p + 1)
                dve.reciprocal(RDEN[:, p % 2], OD[:, 1]).then_inc(rden_ready, 1)
                dve.wait_ge(rden_ready, PAIRS * g + p + 1)
                dve.tensor_tensor(AO[:, par, p], OD[:, 0], RDEN[:, p % 2], ALU.mult).then_inc(attn_ready, 1)

            def step(t, par):
                item = [0]

                def next_max(count=1):
                    for _ in range(count):
                        if there(t + 1):
                            max_item(t + 1, 1 - par, item[0])
                            item[0] += 1

                if there(t + 1):
                    keys16(t + 1)
                if there(t):
                    max_item(t, par, ITEMS - 1)
                if there(t + 2):
                    pool_sums(t + 2, par)
                    pool_reciprocal(slice(0, 2))
                if there(t):
                    divide(t, par, 0)
                if there(t + 1):
                    values(t + 1, 1 - par)
                if there(t - 2):
                    dve.wait_ge(wo_ready, 2 * (t - 1))
                    dve.scalar_tensor_tensor(out=H[:, t - 2], in0=by_pair(bank[4][:, 0:N]), scalar=b_o,
                                             in1=H[:, t - 2], op0=ALU.add, op1=ALU.add).then_inc(out_ready, 1)

                for n in (2, 3):
                    next_max()
                    if there(t + 2):
                        pool_reciprocal(slice(n, n + 1))
                if there(t + 3):
                    pool_max(t + 3, 0)
                    pool_max(t + 3, 1)
                next_max()
                if there(t + 2):
                    pool_ratio(t + 2)
                if there(t - 1):
                    dve.wait_ge(proj_ready, t)
                    dve.scalar_tensor_tensor(out=H[:, t - 1], in0=by_pair(bank[2][:, 0:N]), scalar=b_p,
                                             in1=H[:, t - 1], op0=ALU.add, op1=ALU.add
                                             ).then_inc(h2_ready, 1)
                next_max(2)
                if there(t):
                    divide(t, par, 1)
                next_max()

                next_max(3)
                if there(t - 1):
                    dve.wait_ge(rstd2_ready, t)
                    dve.tensor_tensor(X2[:], bank[4][:, 0:N], NORM2[:], ALU.mult).then_inc(x2_ready, 1)
                next_max()
                if there(t + 2):
                    dve.wait_ge(rstd_ready, t + 3)
                    dve.tensor_tensor(XN[:], by_pair(bank[0][:, 0:N]), by_pair(NORM1[:]), ALU.mult
                                      ).then_inc(xn_ready, 1)
                next_max()
                if there(t):
                    divide(t, par, 2)
                next_max()

                next_max(2)
                if there(t + 3):
                    pool_max(t + 3, 2)
                    pool_max(t + 3, 3)
                next_max(3)
                if there(t):
                    divide(t, par, 3)
                if isinstance(t, int) and t == FIRST:
                    padded_keys()
                    dve.wait_ge(pad_flipped, 1)
                    dve.tensor_copy(pad_rows[:], bank[7][0:HEADS, 0:C]).then_inc(pad_turned, 1)

            setup()
            steps(dve, step)

        @block.tensor
        def _(pe):
            def evacuated(g, s):
                pe.wait_ge(q_ready, 2 * g + s + 1)
                pe.wait_ge(key_ready, 4 * g + 2 * s + 2)

            def pool_raw(g, par, n):
                if n == 0:
                    pe.wait_ge(x_in[par], 8 * (g - par) + 16)
                if n >= 2:
                    pe.wait_ge(exp_ready, PAIRS * g + n - 1)
                    if there(g - 1):
                        pe.wait_ge(xn_ready, g)
                elif there(g - 2):
                    evacuated(g - 2, n)
                elif there(g - 1):
                    pe.wait_ge(exp_ready, PAIRS * (g - 1) + n + 3)
                pe.matmul(bank[n % 2][:, 0:RAW], w_tok, XR[:, par, n], start=True, stop=False,
                          skip_group_check=True).then_inc(raw_ready, 1)

            def pool_shift(g, n):
                pe.wait_ge(max_ready, PAIRS * g + n + 1)
                pe.matmul(bank[n % 2][:, 0:RAW].rearrange("p (k t) -> p k t", k=POOL), neg_id[:],
                          M16[:, n].unsqueeze(1).broadcast_to([128, POOL, T]), start=False, stop=True,
                          skip_group_check=True).then_inc(shift_ready, 1)

            def first_norm_bank(g, n):
                if there(g + 1):
                    pe.wait_ge(exp_ready, PAIRS * (g + 1) + n + 1)
                else:
                    evacuated(g - 1, n)

            def scores(g, par, p, i):
                n = 4 * p + i
                if n == 0:
                    if isinstance(g, int) and g == 0:
                        pe.wait_ge(mx_read, ITEMS - 1)
                    pe.wait_ge(qdiag_in, 16 * HEADS * (g + 1))
                    pe.wait_ge(key_ready, 4 * (g + 1))
                if n % 8 == 0:
                    pe.wait_ge(negmax_in, 16 * (2 * g + n // 8 + 1))
                if n >= 2 or after_first(g):
                    pe.wait_ge(p_ready, 16 * g + n - 1)
                s, qg = 2 * p + i // 2, i % 2
                pe.matmul(bank_s[i % 2][0:C, 0:NB], A[0:ROWS_K + C, par, s, qg],
                          BQ[0:ROWS_K + C, par, s, qg].rearrange("p h c -> p (h c)"), start=True, stop=True
                          ).then_inc(s_ready, 1)

            def max_item(g, par, item):
                bank_max = max_bank(g, item)
                if item == 0:
                    pe.wait_ge(kdiag_in, 16 * HEADS * (g + 1))
                    pe.wait_ge(aq_ready, 4 * (g + 1))
                if isinstance(g, int) and g == 0 and item not in (T0_AT, T0_AT + 1, ITEMS - 1):
                    if item >= 2:
                        pe.wait_ge(mx_read, item - 1)
                elif item or after_first(g):
                    pe.wait_ge(mx_read, ITEMS * g + item)
                if item in (T0_AT, ITEMS - 1):
                    half = int(item > T0_AT)
                    pe.transpose(bank_max[0:32, 0:C], mx[:, par, 32 * half:32 * (half + 1)], ident[0:C, 0:C]
                                 ).then_inc(mx_filled, 1)
                else:
                    m = item - (item > T0_AT)
                    pe.matmul(bank_max[0:C, 0:NB], AQ[0:ROWS_Q + C, m // 2, m % 2],
                              BK[0:ROWS_Q + C, m // 2, m % 2].rearrange("p h c -> p (h c)"), start=True, stop=True
                              ).then_inc(mx_filled, 1)

            def outputs(g, par, p, kind):
                if kind == 0:
                    pe.wait_ge(p_ready, 16 * g + 4 * (p + 1))
                    if p == 0:
                        pe.wait_ge(vm_ready, g + 1)
                    if p or after_first(g):
                        pe.wait_ge(attn_ready, PAIRS * g + p)
                for hh in range(HH):
                    for s in range(2):
                        for qg in range(QG):
                            j = 2 * s + qg
                            at = (2 * p + s) * VB + qg * (VB // 2) + 32 * hh
                            lhs = Vm[:, par, at:at + 32] if kind == 0 else ones_head[hh]
                            mm = pe.matmul(OD[32 * j:32 * (j + 1), kind], lhs,
                                           P[:, p % 2, s, qg, C * hh:C * (hh + 1)], start=(hh == 0),
                                           stop=(hh == HH - 1))
                if kind:
                    mm.then_inc(od_ready, 1)

            def values(g):
                if there(g - 3):
                    pe.wait_ge(r2_ready, PAIRS * (g - 3) + 2)
                if after_first(g):
                    pe.wait_ge(vm_ready, g)
                for n in range(PAIRS):
                    mm = pe.matmul(bank[2][0:C, 128 * n:128 * (n + 1)], XN[:, n], w_v, start=True, stop=True)
                mm.then_inc(v_ready, 1)

            def expert_layer(g, par, l, half):
                if l == 0:
                    pe.wait_ge(r0_ready, 2 * (g + 1))
                    pe.wait_ge(expert_ready, PAIRS * g + 2 * half + 2)
                else:
                    pe.wait_ge(r1_ready, PAIRS * g + 2 * half + 2)
                for n in (2 * half, 2 * half + 1):
                    mm = pe.matmul(bank[2 + 2 * half][:, 2 * C * (n % 2):2 * C * (n % 2 + 1)],
                                   WR[:, par, n, l * WC:l * WC + HID],
                                   (R0, R1)[l][:, n].rearrange("p s c -> p (s c)"), start=True, stop=True)
                mm.then_inc((l1_ready, l2_ready)[l], 1)

            def flat(ap):
                return ap.rearrange("p n c -> p (n c)")

            def step(t, par):
                item = [0]

                def next_max():
                    if there(t + 1):
                        max_item(t + 1, 1 - par, item[0])
                        item[0] += 1

                def scores_of(p, which=range(4)):
                    for i in which:
                        if there(t):
                            scores(t, par, p, i)
                        if p and i % 2:
                            next_max()

                def outputs_of(p, kinds=range(2)):
                    for kind in kinds:
                        if there(t):
                            outputs(t, par, p, kind)

                if isinstance(t, int) and 0 <= t < 2:
                    pe.wait_ge(rows_in[par], 16 * (1 + SLOTS))

                scores_of(0, range(2))
                if there(t + 1):
                    pe.wait_ge(xn_ready, t + 2)
                    for s in range(2):
                        if there(t + 2):
                            pe.wait_ge(exp_ready, PAIRS * (t + 2) + s + 3)
                        pe.matmul(bank[s][:, 0:N], w_qk[s], flat(XN[:]), start=True, stop=True).then_inc(qk_ready, 1)
                scores_of(0, range(2, 4))
                if there(t):
                    max_item(t, par, ITEMS - 1)
                if there(t - 2):
                    for half in range(2):
                        expert_layer(t - 2, par, 1, half)
                outputs_of(0)
                if there(t + 1):
                    if isinstance(t, int) and t == -1:
                        pe.wait_ge(max_rows_in, 16 * (1 + SLOTS))
                        pe.wait_ge(probs_zeroed, 1)
                    values(t + 1)
                if there(t - 2):
                    pe.wait_ge(r2_ready, PAIRS * (t - 1))
                    for s in range(2):
                        pe.matmul(by_pair(bank[4][64 * s:64 * (s + 1), 0:N]), w_o, R2[:, :, s], start=True,
                                  stop=True).then_inc(wo_ready, 1)

                scores_of(1)
                if there(t + 3):
                    pool_raw(t + 3, 1 - par, 0)
                    pool_raw(t + 3, 1 - par, 1)
                next_max()
                if there(t - 1):
                    if there(t + 1):
                        pe.wait_ge(vm_ready, t + 2)
                    pe.wait_ge(attn_ready, PAIRS * t)
                    pe.matmul(bank[2][:, 0:N], w_p, flat(AO[:, 1 - par]), start=True, stop=True
                              ).then_inc(proj_ready, 1)
                outputs_of(1, (0,))
                next_max()
                outputs_of(1, (1,))
                if there(t + 3):
                    pool_shift(t + 3, 0)
                next_max()
                if there(t + 3):
                    pool_shift(t + 3, 1)
                if there(t - 1):
                    if there(t - 2):
                        pe.wait_ge(out_ready, t - 1)
                    pe.wait_ge(h2_ready, t)
                    pe.matmul(bank[4][:, 0:N], centre, flat(H[:, t - 1]), start=True, stop=True
                              ).then_inc(cen2_ready, 1)
                next_max()

                scores_of(2, range(2))
                if there(t + 2):
                    pe.wait_ge(h_ready, t + 3)
                    first_norm_bank(t + 2, 0)
                    pe.matmul(bank[0][:, 0:N], centre, flat(H[:, t + 2]), start=True, stop=True).then_inc(cen_ready, 1)
                scores_of(2, range(2, 4))
                if there(t - 1):
                    pe.wait_ge(sq2_ready, t)
                    pe.matmul(bank[2][:, 0:N], mean, NORM2[:], start=True, stop=True).then_inc(var2_ready, 1)
                if there(t + 2):
                    pe.wait_ge(sq_ready, t + 3)
                    first_norm_bank(t + 2, 1)
                    pe.matmul(bank[1][:, 0:N], mean, NORM1[:], start=True, stop=True).then_inc(var_ready, 1)
                next_max()
                for kind in range(2):
                    outputs_of(2, (kind,))
                    next_max()
                if there(t - 1):
                    pe.wait_ge(x2_ready, t)
                    for s in range(2):
                        pe.matmul(bank[2 + 2 * s][:, 0:N], w_i[s], X2[:], start=True, stop=True).then_inc(wi_ready, 1)
                next_max()

                scores_of(3)
                if there(t + 3):
                    pool_raw(t + 3, 1 - par, 2)
                    pool_raw(t + 3, 1 - par, 3)
                next_max()
                for half in range(2):
                    if there(t - 1):
                        expert_layer(t - 1, 1 - par, 0, half)
                next_max()
                outputs_of(3)
                next_max()
                if there(t + 3):
                    pool_shift(t + 3, 2)
                    pool_shift(t + 3, 3)
                if isinstance(t, int) and t == FIRST:
                    pe.wait_ge(weights_in, 32)
                    pe.wait_ge(pads_zeroed, 1)
                    pe.wait_ge(pad_done, 1)
                    pe.matmul(bank[7][0:HEADS, 0:C], pad_lse[:], cst[0:C, C_FLIP:C_FLIP + C], start=True, stop=True
                              ).then_inc(pad_flipped, 1)

            pe.wait_ge(token_weights_in, 32)
            steps(pe, step)


def prepared(inputs):
    f32 = np.float32
    x = np.asarray(inputs["x"])[:, :RAW].reshape(GROUPS, PAIRS, 2, T, POOL, D)
    xT = np.ascontiguousarray(x.transpose(0, 2, 5, 1, 4, 3)).reshape(GROUPS, 128, PAIRS, RAW)
    qkv, bqkv = np.asarray(inputs["L0_attn_qkv_weight"]), np.asarray(inputs["L0_attn_qkv_bias"])
    w = np.zeros((128, W_ALL), f32)
    for s in range(2):
        rows = slice(64 * s, 64 * (s + 1))
        w[rows, W_TOK + 64 * s:W_TOK + 64 * (s + 1)] = inputs["L0_tok_W"]
        w[rows, W_QK + 128 * s:W_QK + 128 * (s + 1)] = qkv[0:128].T
        w[rows, W_V + 64 * s:W_V + 64 * (s + 1)] = qkv[128:192].T
        w[rows, W_P + 64 * s:W_P + 64 * (s + 1)] = np.asarray(inputs["L0_attn_proj_weight"]).T
        w[rows, W_I + 128 * s:W_I + 128 * (s + 1)] = np.asarray(inputs["L0_ffn_Wi"]).T
        w[rows, W_BIAS + 1] = inputs["L0_attn_proj_bias"]
        w[rows, W_BIAS + 3] = inputs["L0_ffn_bo"]
    w[:, W_O:W_O + D] = np.asarray(inputs["L0_ffn_Wo"]).T
    for l in range(LAYERS):
        w[:, W_S + l * WC:W_S + l * WC + HID] = np.asarray(inputs["L0_ffn_Ws"])[l, 0].T
        w[:, W_S + l * WC + HID] = np.asarray(inputs["L0_ffn_bs"])[l, 0]
    w[:, W_BIAS] = bqkv[0:128]
    w[:, W_BIAS + 2] = inputs["L0_ffn_bi"]
    w[:, W_BV:W_BV + D] = bqkv[None, 128:192]
    wr, br = np.asarray(inputs["L0_ffn_Wr"]), np.asarray(inputs["L0_ffn_br"])
    experts = np.concatenate([wr.transpose(1, 3, 0, 2), br.transpose(1, 2, 0)[..., None]], axis=3)
    experts = np.ascontiguousarray(experts).reshape(wr.shape[1], 128, LAYERS * WC)
    tab = np.ascontiguousarray(np.asarray(inputs["L0_attn_bias_table"]).T)

    half = np.kron(np.eye(2, dtype=f32), np.full((D, D), 1.0 / D, f32))
    c = np.zeros((128, C_ALL), f32)
    c[:, C_CEN:C_CEN + 128] = np.eye(128, dtype=f32) - half
    c[:, C_MEAN:C_MEAN + 128] = half
    c[:, C_ID:C_ID + 128] = np.eye(128, dtype=f32)
    for hh in range(HH):
        c[0:C, C_ONES + 40 * hh:C_ONES + 40 * hh + HD] = 1.0
    c[0:C, C_FLIP:C_FLIP + C] = np.eye(C)[::-1]
    id16 = np.zeros((128, 128 + C), mybir.dt.np(BF16))
    id16[:, 0:128] = -np.eye(128)
    id16[0:C, 128:128 + C] = np.eye(C)[::-1]
    key_rows = np.zeros((C + 1, C), f32)
    key_rows[0, 0:C] = 1.0
    key_rows[1:C, 0:T] = np.eye(T)[::-1]
    key_rows[C, T] = 1.0
    return {"xT": xT, "weights": w, "consts": c, "id16": id16, "key_rows": key_rows,
            "tab": tab, "tab_rev": np.ascontiguousarray(tab[:, ::-1]),
            "experts": experts, "route": np.asarray(inputs["L0_ffn_route_id"]).reshape(1, -1)}


def kernel(**inputs):
    import concourse.bacc as bacc
    from concourse.bass_utils import run_bass_kernel_spmd

    nc = bacc.Bacc("TRN2", target_bir_lowering=False, num_devices=1)
    arrays = prepared(inputs)
    args = [nc.dram_tensor(f"in_{k}", a.shape, mybir.dt.from_np(a.dtype), kind="ExternalInput").ap()
            for k, a in arrays.items()]
    args.append(nc.dram_tensor("outT", (GROUPS, 128, PAIRS, T), F32, kind="ExternalOutput").ap())
    build(nc, *args)
    r = run_bass_kernel_spmd(nc, [{f"in_{k}": a for k, a in arrays.items()}], core_ids=[0])
    out = np.asarray(r.results[0]["outT"]).reshape(GROUPS, 2, D, PAIRS, T)
    return np.ascontiguousarray(out.transpose(0, 3, 1, 4, 2)).reshape(B, T, D)
```

```python
from contextlib import ExitStack

import numpy as np

import concourse.bass as bass
from concourse import mybir

F32 = mybir.dt.float32
BF16 = mybir.dt.bfloat16
I32 = mybir.dt.int32
ACT = mybir.ActivationFunctionType
ALU = mybir.AluOpType
AX_X = mybir.AxisListType.X

B, D = 128, 64
POOL = 4
T = 375 // POOL
WINDOW = 128
PADDED = WINDOW - T
C = T + 1
HEADS, HD = 8, 8
HH, QG = 4, 2
HID, LAYERS = 128, 2
PAIRS = 4
SLOTS = 2 * PAIRS
GROUPS = B // SLOTS
RAW = POOL * T
N = PAIRS * C
NB = HH * C
NT = 2 * WINDOW - 1
WC = HID + 1
ROWS_Q = 32
ROWS_K = 33
VB = HEADS * 40
SUMS = 2 * HD
SCALE = HD ** -0.5
EPS = 1e-5

W_TOK, W_QK, W_V, W_P, W_I, W_O = 0, 128, 384, 512, 768, 1024
W_S = W_O + D
W_BIAS = W_S + LAYERS * WC
W_BV = W_BIAS + 4
W_ALL = W_BV + D
C_CEN, C_MEAN, C_ID, C_FLIP, C_ALL = 0, 128, 256, 384, 384 + C


FIRST, LAST = -3, GROUPS + 1
STEADY = (2, GROUPS - 4)


def steps(eng, step):
    for t in range(FIRST, STEADY[0]):
        step(t, t % 2)
    with eng.Fori(STEADY[0] // 2, STEADY[1] // 2) as i:
        for par in range(2):
            step(2 * i + par, par)
    for t in range(STEADY[1], LAST + 1):
        step(t, t % 2)


def there(group):
    return not isinstance(group, int) or 0 <= group < GROUPS


def after_first(group):
    return not isinstance(group, int) or 0 < group < GROUPS


def build(nc, xT, weights, consts, id16, key_rows, tab, tab_rev, experts, route, outT):
    with ExitStack() as ctx:
        def sb(name, shape, dt=F32):
            return ctx.enter_context(nc.sbuf_tensor(name, shape, dt))

        def sem(name):
            return ctx.enter_context(nc.semaphore(name))

        bank = [ctx.enter_context(nc.psum_tensor(f"bank{i}", [128, 512], F32)) for i in range(8)]

        wts = sb("wts", [128, W_ALL])
        cst = sb("cst", [128, C_ALL])
        neg_id = sb("neg_id", [128, 128], BF16)
        route_sb = sb("route_sb", [1, B // 2], I32)
        bq_scaled = sb("bq_scaled", [64, 1])
        eps_col = sb("eps_col", [128, 1])
        wait_holder = sb("wait_holder", [128, 1])
        shared = sb("shared", [128, LAYERS * WC])
        rel_q16 = sb("rel_q16", [C, HEADS, C], BF16)
        pad_bias = sb("pad_bias", [C, HEADS, PADDED])
        pad_max = sb("pad_max", [C, HEADS])
        pad_sum = sb("pad_sum", [C, HEADS])
        pad_lse = sb("pad_lse", [C, HEADS])
        pad_rows = sb("pad_rows", [HEADS, C])

        H = sb("H", [128, GROUPS, PAIRS, C])
        XN = sb("XN", [128, PAIRS, C])
        AO = sb("AO", [128, 2, PAIRS, 2, C])
        NORM1, NORM2 = sb("NORM1", [128, N]), sb("NORM2", [128, N])

        A = sb("A", [128, 2, SLOTS, QG, C])
        BQ = sb("BQ", [128, 2, SLOTS, QG, HH, C])
        AQ = sb("AQ", [128, SLOTS, QG, C], BF16)
        BK = sb("BK", [128, SLOTS, QG, HH, C], BF16)
        staging = sb("staging", [128, 2, SLOTS * C])
        q_st = staging[0:64].rearrange("p g (s c) -> p g s c", s=SLOTS)
        rel_q = staging[0:C, 0].rearrange("p (h c) -> p h c", h=HEADS)
        rel_k = staging[0:C, 1].rearrange("p (h c) -> p h c", h=HEADS)
        k_st = sb("k_st", [128, SLOTS, C], BF16)
        Vm = sb("Vm", [128, 2, SLOTS * VB])
        P = sb("P", [128, 2, 2, QG, NB])
        mx = sb("mx", [C, 2, SLOTS * HEADS])
        neg_max = sb("neg_max", [32, 2, 2, C])
        RDEN = sb("RDEN", [128, 2, 2, C])

        XR = sb("XR", [128, 2, PAIRS, RAW])
        EX = sb("EX", [128, PAIRS, RAW])
        M16 = sb("M16", [128, PAIRS, T], BF16)
        ND = sb("ND", [128, 2, PAIRS, T])
        RD = sb("RD", [128, PAIRS, T])

        WR = sb("WR", [128, 2, PAIRS, LAYERS * WC])
        R0, R1, R2 = (sb(f"R{i}", [128, PAIRS, 2, C]) for i in range(3))
        X2 = sb("X2", [128, N])

        token_weights_in, weights_in, route_in, bias_in = (
            sem("token_weights_in"), sem("weights_in"), sem("route_in"), sem("bias_in"))
        pad_maxed, pad_shifted, pad_exp, pad_summed, pad_logged, pad_done = (
            sem("pad_maxed"), sem("pad_shifted"), sem("pad_exp"), sem("pad_summed"), sem("pad_logged"),
            sem("pad_done"))
        rel16_cast, rel16_done = sem("rel16_cast"), sem("rel16_done")
        pad_flipped, pad_turned, pad_row_in = sem("pad_flipped"), sem("pad_turned"), sem("pad_row_in")
        max_rows_in, rows_in, small_ready = sem("max_rows_in"), [sem("rows_in0"), sem("rows_in1")], sem("small_ready")
        shared_copied, shared_ready = sem("shared_copied"), sem("shared_ready")
        pads_zeroed, probs_zeroed, bk_zeroed, vm_zeroed, ones_set, bq_zeroed = (
            sem("pads_zeroed"), sem("probs_zeroed"), sem("bk_zeroed"), sem("vm_zeroed"), sem("ones_set"),
            [sem("bq_zeroed0"), sem("bq_zeroed1")])
        x_in = [sem("x_in0"), sem("x_in1")]
        raw_ready, max_ready, shift_ready = sem("raw_ready"), sem("max_ready"), sem("shift_ready")
        exp_ready, prod_ready = sem("exp_ready"), sem("prod_ready")
        half_ready, sums_ready, recip_ready, h_ready = (
            sem("half_ready"), sem("sums_ready"), sem("recip_ready"), sem("h_ready"))
        cen_ready, sq_ready, var_ready, log_ready, rstd_ready, xn_ready = (
            sem("cen_ready"), sem("sq_ready"), sem("var_ready"), sem("log_ready"), sem("rstd_ready"), sem("xn_ready"))
        qk_ready, v_ready, vm_ready = sem("qk_ready"), sem("v_ready"), sem("vm_ready")
        k16_ready, aq_ready, q_ready, key_ready = sem("k16_ready"), sem("aq_ready"), sem("q_ready"), sem("key_ready")
        kdiag_in, qdiag_in, negmax_in = sem("kdiag_in"), sem("qdiag_in"), sem("negmax_in")
        mx_filled, mx_read = sem("mx_filled"), sem("mx_read")
        s_ready, p_ready, od_ready, den_ready, rden_ready, attn_ready = (
            sem("s_ready"), sem("p_ready"), sem("od_ready"), sem("den_ready"), sem("rden_ready"), sem("attn_ready"))
        expert_in, expert_ready = [sem("expert_in0"), sem("expert_in1")], sem("expert_ready")
        proj_ready, h2_ready, cen2_ready, sq2_ready, var2_ready, log2_ready, rstd2_ready, x2_ready = (
            sem("proj_ready"), sem("h2_ready"), sem("cen2_ready"), sem("sq2_ready"), sem("var2_ready"),
            sem("log2_ready"), sem("rstd2_ready"), sem("x2_ready"))
        wi_ready, r0_ready, l1_ready, r1_ready, l2_ready, r2_ready = (
            sem("wi_ready"), sem("r0_ready"), sem("l1_ready"), sem("r1_ready"), sem("l2_ready"), sem("r2_ready"))
        wo_ready, out_ready, out_stored = sem("wo_ready"), sem("out_ready"), sem("out_stored")

        block = ctx.enter_context(nc.Block())
        w_tok, w_v = wts[:, W_TOK:W_TOK + 128], wts[:, W_V:W_V + 128]
        w_p = [wts[:, W_P + 128 * k:W_P + 128 * (k + 1)] for k in range(2)]
        w_qk = [wts[:, W_QK + 128 * s:W_QK + 128 * (s + 1)] for s in range(2)]
        w_i = [wts[:, W_I + 128 * s:W_I + 128 * (s + 1)] for s in range(2)]
        w_o = wts[:, W_O:W_O + D]
        b_qk, b_p, b_i, b_o = (wts[:, W_BIAS + i:W_BIAS + i + 1] for i in range(4))
        b_v = wts[0:C, W_BV:W_BV + D]
        centre, mean, ident = cst[:, C_CEN:C_CEN + 128], cst[:, C_MEAN:C_MEAN + 128], cst[:, C_ID:C_ID + 128]

        bank_s = [bank[5], bank[6]]
        OD = bank[7][:, 0:2 * C].rearrange("p (k c) -> p k c", k=2)

        def by_pair(ap):
            return ap.rearrange("p (n c) -> p n c", n=PAIRS)

        ITEMS, T0_AT = 4 * PAIRS + 2, 10

        def max_bank(g, item):
            return bank_s[0] if isinstance(g, int) and g == 0 and item % 2 and item < ITEMS - 1 else bank[3]

        @block.sync
        def _(sp):
            sp.dma_start(wts[:, W_TOK:W_QK], weights[:, W_TOK:W_QK]).then_inc(token_weights_in, 16)
            sp.dma_start(XR[:, 0], xT[0]).then_inc(x_in[0], 16)
            sp.dma_start(neg_id[:], id16[:, 0:128]).then_inc(token_weights_in, 16)
            sp.dma_start(wts[:, W_QK:W_ALL], weights[:, W_QK:W_ALL]).then_inc(weights_in, 16)
            sp.dma_start(cst[:], consts).then_inc(weights_in, 16)
            sp.dma_start(pad_bias[:], bass.AP(tab_rev.tensor, WINDOW - C + T, [[1, C], [NT, HEADS], [1, PADDED]])
                         ).then_inc(bias_in, 16)
            sp.dma_start(rel_q, bass.AP(tab_rev.tensor, WINDOW - C, [[1, C], [NT, HEADS], [1, C]])
                         ).then_inc(bias_in, 16)
            sp.dma_start(rel_k[0:T], bass.AP(tab.tensor, WINDOW - T, [[1, T], [NT, HEADS], [1, C]])
                         ).then_inc(bias_in, 16)
            sp.dma_start(route_sb[:], route).then_inc(route_in, 16)

            sp.dma_start(AQ[ROWS_Q:ROWS_Q + C].rearrange("p s g c -> p (s g) c"),
                         bass.AP(id16.tensor, 128, [[128 + C, C], [0, SLOTS * QG], [1, C]])).then_inc(max_rows_in, 16)

            def operand_rows(par):
                sp.dma_start(A[32:33 + C, par].rearrange("p s g c -> p (s g) c"),
                             bass.AP(key_rows.tensor, 0, [[C, C + 1], [0, SLOTS * QG], [1, C]])
                             ).then_inc(rows_in[par], 16)
                for s in range(SLOTS):
                    sp.dma_start(BQ[ROWS_K:ROWS_K + C, par, s].rearrange("p g h c -> p (g h) c"), rel_k
                                 ).then_inc(rows_in[par], 16)

            def bias_rows():
                sp.wait_ge(pad_turned, 1)
                sp.dma_start(rel_k[T:C], pad_rows[:]).then_inc(pad_row_in, 16)
                sp.wait_ge(rel16_done, 1)
                for s in range(SLOTS):
                    sp.dma_start(BK[ROWS_Q:ROWS_Q + C, s].rearrange("p g h c -> p (g h) c"), rel_q16[:]
                                 ).then_inc(max_rows_in, 16)
                sp.wait_ge(pad_row_in, 16)
                sp.wait_ge(bias_in, 48)
                operand_rows(0)

            def key_diagonals(g):
                sp.wait_ge(k16_ready, 2 * (g + 1))
                if after_first(g):
                    sp.wait_ge(mx_read, ITEMS * g - 1)
                for h in range(HEADS):
                    hh, qg = h % HH, h // HH
                    sp.dma_start(BK[HD * hh:HD * (hh + 1), :, qg, hh, :], k_st[64 + HD * h:64 + HD * (h + 1)]
                                 ).then_inc(kdiag_in, 16)

            def query_diagonals(g, par):
                sp.wait_ge(q_ready, 2 * (g + 1))
                if isinstance(g, int) and g < 2:
                    sp.wait_ge(bq_zeroed[par], 1)
                for h in range(HEADS):
                    hh, qg = h % HH, h // HH
                    sp.dma_start(BQ[HD * hh:HD * (hh + 1), par, :, qg, hh, :], q_st[HD * h:HD * (h + 1), par]
                                 ).then_inc(qdiag_in, 16)

            def negmax(g, par, half):
                sp.wait_ge(mx_read, ITEMS * g + (ITEMS if half else T0_AT + 1))
                sp.dma_start(BQ[32:33, par, 4 * half:4 * (half + 1)].rearrange("o s g h c -> o (s g h) c"),
                             neg_max[:, par, half]).then_inc(negmax_in, 16)

            def step(t, par):
                if there(t + 1):
                    key_diagonals(t + 1)
                if there(t):
                    negmax(t, par, 1)
                if there(t - 2):
                    sp.wait_ge(out_ready, t - 1)
                    sp.dma_start(outT[t - 2], H[:, t - 2, :, 0:T]).then_inc(out_stored, 16)
                if there(t):
                    if there(t - 2):
                        sp.wait_ge(r2_ready, PAIRS * (t - 1))
                    for n in range(PAIRS):
                        r = sp.value_load(route_sb[0:1, bass.ds(PAIRS * t + n, 1)], min_val=0, max_val=15)
                        sp.dma_start(WR[:, par, n], experts[r]).then_inc(expert_in[par], 16)
                if there(t + 1):
                    query_diagonals(t + 1, 1 - par)
                    if isinstance(t, int) and t == -1:
                        operand_rows(1)
                    negmax(t + 1, 1 - par, 0)
                if there(t + 4):
                    if there(t + 2):
                        sp.wait_ge(sums_ready, 4 * (t + 3))
                    sp.dma_start(XR[:, par], xT[t + 4]).then_inc(x_in[par], 16)
                if isinstance(t, int) and t == FIRST:
                    bias_rows()
                    sp.wait_ge(route_in, 16)
                    sp.wait_ge(bk_zeroed, 1)

            steps(sp, step)
            sp.wait_ge(out_stored, 16 * GROUPS)

        @block.gpsimd
        def _(pool):
            pool.memset(H[:, :, :, T:C], 0.0).then_inc(pads_zeroed, 1)
            pool.wait_ge(pads_zeroed, 1)
            pool.memset(BK[0:32].bitcast(F32), 0.0).then_inc(bk_zeroed, 1)
            pool.wait_ge(bk_zeroed, 1)
            pool.memset(P[64:128], 0.0).then_inc(probs_zeroed, 1)
            pool.wait_ge(probs_zeroed, 1)

            def products(g, par):
                def halve(n):
                    pool.wait_ge(prod_ready, PAIRS * g + n + 1)
                    for summed in (EX[:, n], XR[:, par, n]):
                        pool.tensor_tensor(summed[:, 0:2 * T], summed[:, 0:2 * T], summed[:, 2 * T:4 * T], ALU.add
                                           ).then_inc(half_ready, 1)

                for n in range(PAIRS):
                    pool.wait_ge(exp_ready, PAIRS * g + n + 1)
                    pool.tensor_tensor(XR[:, par, n], XR[:, par, n], EX[:, n], ALU.mult).then_inc(prod_ready, 1)
                    if n % 2:
                        halve(n - 1)
                        halve(n)
                        pairs = slice(n - 1, n + 1)
                        pool.wait_ge(half_ready, 2 * (PAIRS * g + n + 1))
                        for i, summed in ((1, EX[:, pairs]), (0, XR[:, par, pairs])):
                            pool.tensor_tensor(ND[:, i, pairs], summed[:, :, 0:T], summed[:, :, T:2 * T], ALU.add
                                               ).then_inc(sums_ready, 1)

            def ratio(g):
                pool.wait_ge(sums_ready, 4 * (g + 1))
                pool.wait_ge(recip_ready, PAIRS * (g + 1))
                pool.tensor_tensor(H[:, g, :, 0:T], ND[:, 0], RD[:], ALU.mult).then_inc(h_ready, 1)

            def add_shared(g, par):
                pool.wait_ge(expert_in[par], 32 * (g - par) + 64)
                for n in range(PAIRS):
                    pool.tensor_tensor(WR[:, par, n], WR[:, par, n], shared[:], ALU.add).then_inc(expert_ready, 1)

            def step(t, par):
                if there(t + 2):
                    ratio(t + 2)
                if there(t + 3):
                    products(t + 3, 1 - par)
                if there(t):
                    add_shared(t, par)
                if isinstance(t, int) and t == FIRST + 1:
                    for half in range(2):
                        pool.memset(Vm[:, half], 0.0).then_inc(vm_zeroed, 1)
                        pool.wait_ge(vm_zeroed, half + 1)
                        ones = Vm[0:C, half].rearrange("p (n e) -> p n e", e=40)[:, :, SUMS:SUMS + HD]
                        pool.memset(ones, 1.0).then_inc(ones_set, 1)
                    pool.wait_ge(ones_set, 2)
                    pool.wait_ge(weights_in, 32)
                    pool.tensor_copy(shared[:], wts[:, W_S:W_S + LAYERS * WC]).then_inc(shared_copied, 1)
                    pool.wait_ge(shared_copied, 1)
                    for l in range(LAYERS):
                        m = shared[:, l * WC:l * WC + HID]
                        pool.tensor_tensor(m, m, ident, ALU.add).then_inc(shared_ready, 1)
                    pool.wait_ge(shared_ready, 2)
                if isinstance(t, int) and t == -1:
                    pool.memset(BQ[0:32, 1], 0.0).then_inc(bq_zeroed[1], 1)
                    pool.wait_ge(bq_zeroed[1], 1)

            steps(pool, step)

        @block.scalar
        def _(act):
            act.preload_act_table_set("natural_log_exp_and_others")

            def squares(cen, bank_c, norm, sq, g):
                act.wait_ge(cen, g + 1)
                act.activation(norm[:], bank_c[:, 0:N], ACT.Square).then_inc(sq, 1)

            def inverse_deviation(var, bank_v, norm, log, rstd, g):
                act.wait_ge(var, g + 1)
                act.activation(norm[:], bank_v[:, 0:N], ACT.Ln, bias=eps_col[:]).then_inc(log, 1)
                act.wait_ge(log, g + 1)
                act.activation(norm[:], norm[:], ACT.Exp, scale=-0.5).then_inc(rstd, 1)

            def pool_exp(g, n):
                act.wait_ge(shift_ready, PAIRS * g + n + 1)
                if after_first(g):
                    act.wait_ge(sums_ready, 4 * g)
                act.activation(EX[:, n], bank[n % 2][:, 0:RAW], ACT.Exp).then_inc(exp_ready, 1)

            def padded_keys():
                act.wait_ge(pad_shifted, 1)
                act.activation(pad_bias[:], pad_bias[:], ACT.Exp).then_inc(pad_exp, 1)
                act.wait_ge(pad_summed, 1)
                act.activation(pad_sum[:], pad_sum[:], ACT.Ln).then_inc(pad_logged, 1)

            def queries(g, par, i):
                if i < 4:
                    s, qg = i // 2, i % 2
                    act.wait_ge(qk_ready, 2 * g + s + 1)
                    if i == 0 and after_first(g):
                        act.wait_ge(mx_read, ITEMS * g - 1)
                    act.activation(AQ[0:32, s:SLOTS:2, qg, :], by_pair(bank[s][32 * qg:32 * (qg + 1), 0:N]),
                                   ACT.Identity, bias=bq_scaled[32 * qg:32 * (qg + 1)], scale=SCALE
                                   ).then_inc(aq_ready, 1)
                else:
                    s = i - 4
                    act.activation(q_st[:, par, s:SLOTS:2, :], by_pair(bank[s][0:64, 0:N]), ACT.Identity,
                                   bias=bq_scaled[:], scale=SCALE).then_inc(q_ready, 1)

            def keys(g, par, s):
                act.wait_ge(k16_ready, 2 * g + s + 1)
                for qg in range(QG):
                    rows = slice(64 + 32 * qg, 96 + 32 * qg)
                    act.activation(A[0:32, par, s:SLOTS:2, qg, :], by_pair(bank[s][rows, 0:N]),
                                   ACT.Identity, bias=b_qk[rows]).then_inc(key_ready, 1)

            def exps(t, p, which):
                for i in which:
                    if there(t):
                        act.wait_ge(s_ready, 16 * t + 4 * p + i + 1)
                        if p >= 2 or after_first(t):
                            act.wait_ge(od_ready, PAIRS * t + p - 1)
                        act.activation(P[0:C, p % 2, i // 2, i % 2], bank_s[i % 2][0:C, 0:NB], ACT.Exp
                                       ).then_inc(p_ready, 1)

            def step(t, par):
                for i in range(4):
                    exps(t, 0, (i,))
                    if there(t + 1):
                        for evac in ((), (0, 1), (), (2, 3))[i]:
                            queries(t + 1, 1 - par, evac)
                if there(t - 2):
                    for n in range(PAIRS):
                        act.wait_ge(l2_ready, 2 * (t - 2) + n // 2 + 1)
                        act.activation(R2[:, n].rearrange("p s c -> p (s c)"),
                                       bank[2 + 2 * (n // 2)][:, 2 * C * (n % 2):2 * C * (n % 2 + 1)],
                                       ACT.Relu, bias=WR[:, par, n, WC + HID:2 * WC]).then_inc(r2_ready, 1)
                if there(t + 1):
                    queries(t + 1, 1 - par, 4)
                    queries(t + 1, 1 - par, 5)
                    keys(t + 1, 1 - par, 0)

                exps(t, 1, range(2))
                if there(t + 1):
                    keys(t + 1, 1 - par, 1)
                exps(t, 1, range(2, 4))
                if there(t + 3):
                    pool_exp(t + 3, 0)
                    pool_exp(t + 3, 1)
                if there(t - 1):
                    squares(cen2_ready, bank[4], NORM2, sq2_ready, t - 1)

                exps(t, 2, range(2))
                if there(t + 2):
                    squares(cen_ready, bank[0], NORM1, sq_ready, t + 2)
                exps(t, 2, range(2, 4))
                if there(t - 1):
                    inverse_deviation(var2_ready, bank[2], NORM2, log2_ready, rstd2_ready, t - 1)
                if there(t + 2):
                    inverse_deviation(var_ready, bank[1], NORM1, log_ready, rstd_ready, t + 2)
                if there(t - 1):
                    for s in range(2):
                        act.wait_ge(wi_ready, 2 * (t - 1) + s + 1)
                        act.activation(R0[:, :, s], by_pair(bank[2 + 2 * s][:, 0:N]), ACT.Relu, bias=b_i
                                       ).then_inc(r0_ready, 1)

                exps(t, 3, range(4))
                if there(t + 3):
                    pool_exp(t + 3, 2)
                    pool_exp(t + 3, 3)
                if there(t - 1):
                    for n in range(PAIRS):
                        act.wait_ge(l1_ready, 2 * (t - 1) + n // 2 + 1)
                        act.activation(R1[:, n].rearrange("p s c -> p (s c)"),
                                       bank[2 + 2 * (n // 2)][:, 2 * C * (n % 2):2 * C * (n % 2 + 1)],
                                       ACT.Relu, bias=WR[:, 1 - par, n, HID:WC]).then_inc(r1_ready, 1)
                if isinstance(t, int) and t == FIRST:
                    padded_keys()
                if isinstance(t, int) and t == -2:
                    act.wait_ge(small_ready, 2)
                    act.wait_ge(rel16_cast, 1)
                    act.wait_ge(probs_zeroed, 1)
                if isinstance(t, int) and t == -1:
                    for par in range(2):
                        act.wait_ge(rows_in[par], 16 * (1 + SLOTS))

            steps(act, step)

        @block.vector
        def _(dve):
            def setup():
                dve.memset(eps_col[:], EPS).then_inc(small_ready, 1)
                dve.memset(BQ[0:32, 0], 0.0).then_inc(bq_zeroed[0], 1)

            def padded_keys():
                dve.wait_ge(weights_in, 32)
                dve.tensor_scalar(bq_scaled[:], b_qk[0:64], SCALE, None, ALU.mult).then_inc(small_ready, 1)
                dve.wait_ge(bias_in, 48)
                dve.tensor_reduce(pad_max[:], pad_bias[:], AX_X, ALU.max).then_inc(pad_maxed, 1)
                dve.wait_ge(pad_maxed, 1)
                dve.tensor_tensor(pad_bias[:], pad_bias[:], pad_max[:].unsqueeze(2).broadcast_to([C, HEADS, PADDED]),
                                  ALU.subtract).then_inc(pad_shifted, 1)
                dve.tensor_copy(rel_q16[:], rel_q).then_inc(rel16_cast, 1)
                dve.wait_ge(pad_exp, 1)
                dve.tensor_reduce(pad_sum[:], pad_bias[:], AX_X, ALU.add).then_inc(pad_summed, 1)
                dve.wait_ge(pad_logged, 1)
                dve.tensor_tensor(pad_lse[:], pad_sum[:], pad_max[:], ALU.add).then_inc(pad_done, 1)
                dve.wait_ge(pad_done, 1)
                dve.wait_ge(rel16_cast, 1)
                dve.tensor_copy(rel_q16[:, :, T:T + 1], pad_lse[:].unsqueeze(2)).then_inc(rel16_done, 1)

            def pool_max(g, n):
                dve.wait_ge(raw_ready, PAIRS * g + n + 1)
                dve.tensor_reduce(M16[:, n], bank[n % 2][:, 0:RAW].rearrange("p (k t) -> p t k", k=POOL), AX_X,
                                  ALU.max).then_inc(max_ready, 1)

            def pool_reciprocal(g, n):
                if n % 2 == 0:
                    dve.wait_ge(sums_ready, 4 * g + n + 2)
                if n == 0 and after_first(g):
                    dve.wait_ge(h_ready, g)
                dve.reciprocal(RD[:, n], ND[:, 1, n]).then_inc(recip_ready, 1)

            def keys16(g):
                for s in range(2):
                    dve.wait_ge(qk_ready, 2 * g + s + 1)
                    dve.tensor_scalar(k_st[64:128, s:SLOTS:2, :], by_pair(bank[s][:, 0:N])[64:128], b_qk[64:128], None,
                                      ALU.add).then_inc(k16_ready, 1)

            def values(g, par):
                if isinstance(g, int) and g < 2:
                    dve.wait_ge(ones_set, g + 1)
                dve.wait_ge(v_ready, g + 1)
                dve.tensor_tensor(
                    Vm[0:C, par].rearrange("p (s h e) -> p s h e", s=SLOTS, e=40)[:, :, :, 0:HD],
                    bank[2][0:C, :].rearrange("p (s h e) -> p s h e", s=SLOTS, h=HEADS),
                    b_v.rearrange("p (h e) -> p h e", h=HEADS).unsqueeze(1).broadcast_to([C, SLOTS, HEADS, HD]),
                    ALU.add).then_inc(vm_ready, 1)

            def max_item(g, par, item):
                bank_max = max_bank(g, item)
                dve.wait_ge(mx_filled, ITEMS * g + item + 1)
                if item in (T0_AT, ITEMS - 1):
                    dve.tensor_scalar(neg_max[:, par, int(item > T0_AT)], bank_max[0:32, 0:C], -1.0, None, ALU.mult
                                      ).then_inc(mx_read, 1)
                else:
                    m = item - (item > T0_AT)
                    dve.tensor_reduce(mx[:, par, HH * m:HH * (m + 1)],
                                      bank_max[0:C, 0:NB].rearrange("p (h c) -> p h c", h=HH)[:, :, 0:C], AX_X,
                                      ALU.max).then_inc(mx_read, 1)

            def divide(g, par, p, part):
                den = RDEN[:, p % 2]
                if part == 0:
                    dve.wait_ge(od_ready, PAIRS * g + p + 1)
                    dve.memset(wait_holder[:], 0.0)
                    dve.stream_shuffle(den, OD, [SUMS + i % SUMS for i in range(32)]).then_inc(den_ready, 1)
                    dve.wait_ge(den_ready, PAIRS * g + p + 1)
                dve.reciprocal(den[:, part], den[:, part]).then_inc(rden_ready, 1)
                if part == 1:
                    dve.wait_ge(rden_ready, 2 * (PAIRS * g + p + 1))
                    dve.tensor_tensor(AO[:, par, p], OD, den, ALU.mult).then_inc(attn_ready, 1)

            def step(t, par):
                item = [0]

                def next_max(count=1):
                    for _ in range(count):
                        if there(t + 1):
                            max_item(t + 1, 1 - par, item[0])
                            item[0] += 1

                filling = isinstance(t, int) and t < 0

                def divide_pair(p, part):
                    if there(t):
                        divide(t, par, p, part)

                if there(t + 1):
                    keys16(t + 1)
                if there(t):
                    max_item(t, par, ITEMS - 2)
                if there(t - 1):
                    for part in range(2):
                        divide(t - 1, 1 - par, 3, part)
                if there(t):
                    max_item(t, par, ITEMS - 1)
                if there(t + 2):
                    pool_reciprocal(t + 2, 2)
                divide_pair(0, 0)
                divide_pair(0, 1)
                if there(t + 1):
                    values(t + 1, 1 - par)
                if there(t - 2):
                    dve.wait_ge(wo_ready, 2 * (t - 1))
                    dve.scalar_tensor_tensor(out=H[:, t - 2], in0=by_pair(bank[4][:, 0:N]), scalar=b_o,
                                             in1=H[:, t - 2], op0=ALU.add, op1=ALU.add).then_inc(out_ready, 1)

                next_max()
                if there(t + 2):
                    pool_reciprocal(t + 2, 3)
                next_max()
                if there(t + 3):
                    pool_max(t + 3, 0)
                    pool_max(t + 3, 1)
                next_max(2)
                if there(t - 1):
                    dve.wait_ge(proj_ready, t)
                    dve.scalar_tensor_tensor(out=H[:, t - 1], in0=by_pair(bank[2][:, 0:N]), scalar=b_p,
                                             in1=H[:, t - 1], op0=ALU.add, op1=ALU.add
                                             ).then_inc(h2_ready, 1)
                next_max()
                divide_pair(1, 0)
                next_max()

                divide_pair(1, 1)
                next_max(3)
                if there(t - 1):
                    dve.wait_ge(rstd2_ready, t)
                    dve.tensor_tensor(X2[:], bank[4][:, 0:N], NORM2[:], ALU.mult).then_inc(x2_ready, 1)
                next_max()
                if there(t + 2):
                    dve.wait_ge(rstd_ready, t + 3)
                    dve.tensor_tensor(XN[:], by_pair(bank[0][:, 0:N]), by_pair(NORM1[:]), ALU.mult
                                      ).then_inc(xn_ready, 1)
                divide_pair(2, 0)
                next_max()
                divide_pair(2, 1)

                for n in range(2):
                    next_max()
                    if there(t + 3) and not filling:
                        pool_reciprocal(t + 3, n)
                if there(t + 3):
                    pool_max(t + 3, 2)
                    pool_max(t + 3, 3)
                next_max(2)
                next_max()
                if isinstance(t, int) and t == FIRST:
                    padded_keys()
                    dve.wait_ge(pad_flipped, 1)
                    dve.tensor_copy(pad_rows[:], bank[7][0:HEADS, 0:C]).then_inc(pad_turned, 1)
                if filling:
                    for n in range(2):
                        pool_reciprocal(t + 3, n)

            setup()
            steps(dve, step)

        @block.tensor
        def _(pe):
            def evacuated(g, s):
                pe.wait_ge(q_ready, 2 * g + s + 1)
                pe.wait_ge(key_ready, 4 * g + 2 * s + 2)

            def pool_raw(g, par, n):
                if n == 0:
                    pe.wait_ge(x_in[par], 8 * (g - par) + 16)
                if n >= 2:
                    pe.wait_ge(exp_ready, PAIRS * g + n - 1)
                    if there(g - 1):
                        pe.wait_ge(xn_ready, g)
                elif there(g - 2):
                    evacuated(g - 2, n)
                elif there(g - 1):
                    pe.wait_ge(exp_ready, PAIRS * (g - 1) + n + 3)
                pe.matmul(bank[n % 2][:, 0:RAW], w_tok, XR[:, par, n], start=True, stop=False,
                          skip_group_check=True).then_inc(raw_ready, 1)

            def pool_shift(g, n):
                pe.wait_ge(max_ready, PAIRS * g + n + 1)
                pe.matmul(bank[n % 2][:, 0:RAW].rearrange("p (k t) -> p k t", k=POOL), neg_id[:],
                          M16[:, n].unsqueeze(1).broadcast_to([128, POOL, T]), start=False, stop=True,
                          skip_group_check=True).then_inc(shift_ready, 1)

            def first_norm_bank(g, n):
                if there(g + 1):
                    pe.wait_ge(exp_ready, PAIRS * (g + 1) + n + 1)
                else:
                    evacuated(g - 1, n)

            def scores(g, par, p, i):
                n = 4 * p + i
                if n == 0:
                    if isinstance(g, int) and g == 0:
                        pe.wait_ge(mx_read, ITEMS - 2)
                    pe.wait_ge(qdiag_in, 16 * HEADS * (g + 1))
                    pe.wait_ge(key_ready, 4 * (g + 1))
                if n % 8 == 0:
                    pe.wait_ge(negmax_in, 16 * (2 * g + n // 8 + 1))
                if n >= 2 or after_first(g):
                    pe.wait_ge(p_ready, 16 * g + n - 1)
                s, qg = 2 * p + i // 2, i % 2
                pe.matmul(bank_s[i % 2][0:C, 0:NB], A[0:ROWS_K + C, par, s, qg],
                          BQ[0:ROWS_K + C, par, s, qg].rearrange("p h c -> p (h c)"), start=True, stop=True
                          ).then_inc(s_ready, 1)

            def max_item(g, par, item):
                bank_max = max_bank(g, item)
                if item == 0:
                    pe.wait_ge(kdiag_in, 16 * HEADS * (g + 1))
                    pe.wait_ge(aq_ready, 4 * (g + 1))
                if isinstance(g, int) and g == 0 and item not in (T0_AT, T0_AT + 1, ITEMS - 1):
                    if item >= 2:
                        pe.wait_ge(mx_read, item - 1)
                elif item or after_first(g):
                    pe.wait_ge(mx_read, ITEMS * g + item)
                if item in (T0_AT, ITEMS - 1):
                    half = int(item > T0_AT)
                    pe.transpose(bank_max[0:32, 0:C], mx[:, par, 32 * half:32 * (half + 1)], ident[0:C, 0:C]
                                 ).then_inc(mx_filled, 1)
                else:
                    m = item - (item > T0_AT)
                    pe.matmul(bank_max[0:C, 0:NB], AQ[0:ROWS_Q + C, m // 2, m % 2],
                              BK[0:ROWS_Q + C, m // 2, m % 2].rearrange("p h c -> p (h c)"), start=True, stop=True
                              ).then_inc(mx_filled, 1)

            def outputs(g, par, p):
                pe.wait_ge(p_ready, 16 * g + 4 * (p + 1))
                if p == 0:
                    pe.wait_ge(vm_ready, g + 1)
                if p or after_first(g):
                    pe.wait_ge(attn_ready, PAIRS * g + p)
                for hh in range(HH):
                    for s in range(2):
                        for qg in range(QG):
                            j, k, a = 2 * s + qg, hh // 2, hh % 2
                            at = (2 * p + s) * VB + 80 * (2 * qg + k) + 32 * a
                            mm = pe.matmul(OD[32 * j:32 * (j + 1), k], Vm[:, par, at:at + 32],
                                           P[:, p % 2, s, qg, C * hh:C * (hh + 1)], start=(a == 0), stop=(a == 1))
                mm.then_inc(od_ready, 1)

            def values(g):
                if there(g - 3):
                    pe.wait_ge(r2_ready, PAIRS * (g - 3) + 2)
                if after_first(g):
                    pe.wait_ge(vm_ready, g)
                for n in range(PAIRS):
                    mm = pe.matmul(bank[2][0:C, 128 * n:128 * (n + 1)], XN[:, n], w_v, start=True, stop=True)
                mm.then_inc(v_ready, 1)

            def expert_layer(g, par, l, half):
                if l == 0:
                    pe.wait_ge(r0_ready, 2 * (g + 1))
                    pe.wait_ge(expert_ready, PAIRS * g + 2 * half + 2)
                else:
                    pe.wait_ge(r1_ready, PAIRS * g + 2 * half + 2)
                for n in (2 * half, 2 * half + 1):
                    mm = pe.matmul(bank[2 + 2 * half][:, 2 * C * (n % 2):2 * C * (n % 2 + 1)],
                                   WR[:, par, n, l * WC:l * WC + HID],
                                   (R0, R1)[l][:, n].rearrange("p s c -> p (s c)"), start=True, stop=True)
                mm.then_inc((l1_ready, l2_ready)[l], 1)

            def flat(ap):
                return ap.rearrange("p n c -> p (n c)")

            def step(t, par):
                item = [0]

                def next_max():
                    if there(t + 1):
                        max_item(t + 1, 1 - par, item[0])
                        item[0] += 1

                def scores_of(p, which=range(4)):
                    for i in which:
                        if there(t):
                            scores(t, par, p, i)
                        if p and i % 2:
                            next_max()

                def outputs_of(p):
                    if there(t):
                        outputs(t, par, p)

                if there(t + 1):
                    pe.wait_ge(xn_ready, t + 2)
                    for s in range(2):
                        if there(t + 2):
                            pe.wait_ge(exp_ready, PAIRS * (t + 2) + s + 3)
                        pe.matmul(bank[s][:, 0:N], w_qk[s], flat(XN[:]), start=True, stop=True).then_inc(qk_ready, 1)
                scores_of(0, range(1))
                if there(t):
                    max_item(t, par, ITEMS - 2)
                scores_of(0, range(1, 4))
                if there(t):
                    max_item(t, par, ITEMS - 1)
                if there(t - 2):
                    for half in range(2):
                        expert_layer(t - 2, par, 1, half)
                outputs_of(0)
                if there(t + 1):
                    if isinstance(t, int) and t == -1:
                        pe.wait_ge(max_rows_in, 16 * (1 + SLOTS))
                        pe.wait_ge(probs_zeroed, 1)
                    values(t + 1)
                if there(t - 2):
                    pe.wait_ge(r2_ready, PAIRS * (t - 1))
                    for s in range(2):
                        pe.matmul(by_pair(bank[4][64 * s:64 * (s + 1), 0:N]), w_o, R2[:, :, s], start=True,
                                  stop=True).then_inc(wo_ready, 1)

                scores_of(1)
                if there(t + 3):
                    pool_raw(t + 3, 1 - par, 0)
                    pool_raw(t + 3, 1 - par, 1)
                next_max()
                if there(t - 1):
                    if there(t + 1):
                        pe.wait_ge(vm_ready, t + 2)
                    pe.wait_ge(attn_ready, PAIRS * t)
                    for k in range(2):
                        mm = pe.matmul(by_pair(bank[2][:, 0:N]), w_p[k], AO[:, 1 - par, :, k], start=(k == 0),
                                       stop=(k == 1))
                    mm.then_inc(proj_ready, 1)
                next_max()
                outputs_of(1)
                next_max()
                if there(t + 3):
                    pool_shift(t + 3, 0)
                    pool_shift(t + 3, 1)
                if there(t - 1):
                    if there(t - 2):
                        pe.wait_ge(out_ready, t - 1)
                    pe.wait_ge(h2_ready, t)
                    pe.matmul(bank[4][:, 0:N], centre, flat(H[:, t - 1]), start=True, stop=True
                              ).then_inc(cen2_ready, 1)
                next_max()

                scores_of(2, range(2))
                if there(t + 2):
                    pe.wait_ge(h_ready, t + 3)
                    first_norm_bank(t + 2, 0)
                    pe.matmul(bank[0][:, 0:N], centre, flat(H[:, t + 2]), start=True, stop=True).then_inc(cen_ready, 1)
                scores_of(2, range(2, 4))
                if there(t - 1):
                    pe.wait_ge(sq2_ready, t)
                    pe.matmul(bank[2][:, 0:N], mean, NORM2[:], start=True, stop=True).then_inc(var2_ready, 1)
                if there(t + 2):
                    pe.wait_ge(sq_ready, t + 3)
                    first_norm_bank(t + 2, 1)
                    pe.matmul(bank[1][:, 0:N], mean, NORM1[:], start=True, stop=True).then_inc(var_ready, 1)
                next_max()
                outputs_of(2)
                next_max()
                if there(t - 1):
                    pe.wait_ge(x2_ready, t)
                    for s in range(2):
                        pe.matmul(bank[2 + 2 * s][:, 0:N], w_i[s], X2[:], start=True, stop=True).then_inc(wi_ready, 1)
                next_max()

                scores_of(3)
                if there(t + 3):
                    pool_raw(t + 3, 1 - par, 2)
                    pool_raw(t + 3, 1 - par, 3)
                next_max()
                for half in range(2):
                    if there(t - 1):
                        expert_layer(t - 1, 1 - par, 0, half)
                next_max()
                if there(t + 3):
                    pool_shift(t + 3, 2)
                    pool_shift(t + 3, 3)
                outputs_of(3)
                next_max()
                if isinstance(t, int) and t == FIRST:
                    pe.wait_ge(weights_in, 32)
                    pe.wait_ge(pads_zeroed, 1)
                    pe.wait_ge(pad_done, 1)
                    pe.matmul(bank[7][0:HEADS, 0:C], pad_lse[:], cst[0:C, C_FLIP:C_FLIP + C], start=True, stop=True
                              ).then_inc(pad_flipped, 1)

            pe.wait_ge(token_weights_in, 32)
            steps(pe, step)


def prepared(inputs):
    f32 = np.float32
    x = np.asarray(inputs["x"])[:, :RAW].reshape(GROUPS, PAIRS, 2, T, POOL, D)
    xT = np.ascontiguousarray(x.transpose(0, 2, 5, 1, 4, 3)).reshape(GROUPS, 128, PAIRS, RAW)
    qkv, bqkv = np.asarray(inputs["L0_attn_qkv_weight"]), np.asarray(inputs["L0_attn_qkv_bias"])
    w = np.zeros((128, W_ALL), f32)
    for s in range(2):
        rows = slice(64 * s, 64 * (s + 1))
        w[rows, W_TOK + 64 * s:W_TOK + 64 * (s + 1)] = inputs["L0_tok_W"]
        w[rows, W_QK + 128 * s:W_QK + 128 * (s + 1)] = qkv[0:128].T
        w[rows, W_V + 64 * s:W_V + 64 * (s + 1)] = qkv[128:192].T
        proj = np.asarray(inputs["L0_attn_proj_weight"]).T.reshape(QG, 2, 2 * HD, D)
        for qg in range(QG):
            at = 64 * s + 32 * qg
            for k in range(2):
                w[at:at + 2 * HD, W_P + 128 * k + 64 * s:W_P + 128 * k + 64 * (s + 1)] = proj[qg, k]
        w[rows, W_I + 128 * s:W_I + 128 * (s + 1)] = np.asarray(inputs["L0_ffn_Wi"]).T
        w[rows, W_BIAS + 1] = inputs["L0_attn_proj_bias"]
        w[rows, W_BIAS + 3] = inputs["L0_ffn_bo"]
    w[:, W_O:W_O + D] = np.asarray(inputs["L0_ffn_Wo"]).T
    for l in range(LAYERS):
        w[:, W_S + l * WC:W_S + l * WC + HID] = np.asarray(inputs["L0_ffn_Ws"])[l, 0].T
        w[:, W_S + l * WC + HID] = np.asarray(inputs["L0_ffn_bs"])[l, 0]
    w[:, W_BIAS] = bqkv[0:128]
    w[:, W_BIAS + 2] = inputs["L0_ffn_bi"]
    w[:, W_BV:W_BV + D] = bqkv[None, 128:192]
    wr, br = np.asarray(inputs["L0_ffn_Wr"]), np.asarray(inputs["L0_ffn_br"])
    experts = np.concatenate([wr.transpose(1, 3, 0, 2), br.transpose(1, 2, 0)[..., None]], axis=3)
    experts = np.ascontiguousarray(experts).reshape(wr.shape[1], 128, LAYERS * WC)
    tab = np.ascontiguousarray(np.asarray(inputs["L0_attn_bias_table"]).T)

    half = np.kron(np.eye(2, dtype=f32), np.full((D, D), 1.0 / D, f32))
    c = np.zeros((128, C_ALL), f32)
    c[:, C_CEN:C_CEN + 128] = np.eye(128, dtype=f32) - half
    c[:, C_MEAN:C_MEAN + 128] = half
    c[:, C_ID:C_ID + 128] = np.eye(128, dtype=f32)
    c[0:C, C_FLIP:C_FLIP + C] = np.eye(C)[::-1]
    id16 = np.zeros((128, 128 + C), mybir.dt.np(BF16))
    id16[:, 0:128] = -np.eye(128)
    id16[0:C, 128:128 + C] = np.eye(C)[::-1]
    key_rows = np.zeros((C + 1, C), f32)
    key_rows[0, 0:C] = 1.0
    key_rows[1:C, 0:T] = np.eye(T)[::-1]
    key_rows[C, T] = 1.0
    return {"xT": xT, "weights": w, "consts": c, "id16": id16, "key_rows": key_rows,
            "tab": tab, "tab_rev": np.ascontiguousarray(tab[:, ::-1]),
            "experts": experts, "route": np.asarray(inputs["L0_ffn_route_id"]).reshape(1, -1)}


def kernel(**inputs):
    import concourse.bacc as bacc
    from concourse.bass_utils import run_bass_kernel_spmd

    nc = bacc.Bacc("TRN2", target_bir_lowering=False, num_devices=1)
    arrays = prepared(inputs)
    args = [nc.dram_tensor(f"in_{k}", a.shape, mybir.dt.from_np(a.dtype), kind="ExternalInput").ap()
            for k, a in arrays.items()]
    args.append(nc.dram_tensor("outT", (GROUPS, 128, PAIRS, T), F32, kind="ExternalOutput").ap())
    build(nc, *args)
    r = run_bass_kernel_spmd(nc, [{f"in_{k}": a for k, a in arrays.items()}], core_ids=[0])
    out = np.asarray(r.results[0]["outT"]).reshape(GROUPS, 2, D, PAIRS, T)
    return np.ascontiguousarray(out.transpose(0, 3, 1, 4, 2)).reshape(B, T, D)
```
